# Optimizing a Trainium2 kernel written in Bass

```python
import numpy as np
import jax
import jax.numpy as jnp

def _softmax(x, axis=-1):
    return jax.nn.softmax(x, axis=axis)

def _gelu(x):
    return jax.nn.gelu(x, approximate=True)

def _silu(x):
    return jax.nn.silu(x)

def _sigmoid(x):
    return jax.nn.sigmoid(x)

def _layernorm(x, axis=-1, eps=1e-05):
    m = jnp.mean(x, axis=axis, keepdims=True)
    v = jnp.var(x, axis=axis, keepdims=True)
    return (x - m) / jnp.sqrt(v + eps)

def _scatter_add(tgt, idx, src, axis=0):
    return tgt.at[idx].add(src)

def _segment_sum(src, seg, n):
    return jax.ops.segment_sum(src, seg, n)
kernel_name = 'mk_adj_resnorm_d2_adj_r2_d04b25'

def setup_inputs(seed: int=0):
    np.random.seed(seed)
    _w = jnp.asarray

    def _rec_inputs():
        import jax
        import jax.numpy as jnp
        _gk = jax.random.key(seed)
        x = -0.0001538 + 1 * jax.random.normal(jax.random.fold_in(_gk, 1), (64, 128, 384), jnp.float32)
        _a = jax.random.bernoulli(jax.random.fold_in(_gk, 2), 0.125, (64, 128, 128))
        _a = jnp.logical_or(_a, jnp.swapaxes(_a, -1, -2))
        _a = jnp.logical_or(_a, jnp.eye(128, dtype=bool))
        _af = _a.astype(jnp.float32)
        _af = _af * jax.random.uniform(jax.random.fold_in(_gk, 3), (64, 128, 128), jnp.float32, 0.05, 4.42607)
        adj = _af
        return (x, adj)
    x, adj = _rec_inputs()

    def _L0_gnn_setup():
        import jax, jax.numpy as jnp
        import numpy as np
        NUM_HEADS = 12
        HIDDEN = 384
        HEAD = HIDDEN // NUM_HEADS
        SCALE = HIDDEN ** (-0.5)
        key = jax.random.key(seed)
        ks = jax.random.split(key, 8)
        B, N = (16, 256)
        std = HIDDEN ** (-0.5)
        return {'x': jax.random.normal(ks[0], (B, N, HIDDEN), dtype=jnp.float32), 'encoding_bias': jax.random.normal(ks[1], (B, N, N), dtype=jnp.float32), 'Wq': jax.random.normal(ks[2], (HIDDEN, HIDDEN), dtype=jnp.float32) * std, 'Wk': jax.random.normal(ks[3], (HIDDEN, HIDDEN), dtype=jnp.float32) * std, 'Wv': jax.random.normal(ks[4], (HIDDEN, HIDDEN), dtype=jnp.float32) * std, 'bv': jax.random.normal(ks[5], (HIDDEN,), dtype=jnp.float32) * 0.01, 'Wo': jax.random.normal(ks[6], (HIDDEN, HIDDEN), dtype=jnp.float32) * std, 'bo': jax.random.normal(ks[7], (HIDDEN,), dtype=jnp.float32) * 0.01}
    _L0_gnn_all = _L0_gnn_setup()
    _L0_gnn_in = {k: v for k, v in _L0_gnn_all.items() if k in ('Wq', 'Wk', 'Wv', 'bv', 'Wo', 'bo')}
    del _L0_gnn_all

    def _L1_gnn_setup():
        import jax, jax.numpy as jnp
        import numpy as np
        D_MODEL = 384
        NHEADS = 8
        D_FF = 1536
        B, N = (8, 512)
        EPS = 1e-06

        def _rmsnorm(x, alpha, gamma):
            x = x * jax.lax.rsqrt(jnp.mean(x * x, axis=-1, keepdims=True) + EPS)
            return alpha * x + gamma
        key = jax.random.key(seed)
        ks = jax.random.split(key, 10)
        d, f = (D_MODEL, D_FF)
        s = 1.0 / np.sqrt(d)
        inp = {'x': jax.random.normal(ks[0], (B, N, d), dtype=jnp.float32), 'attn_bias': jax.random.normal(ks[1], (B, N, N), dtype=jnp.float32), 'wq': jax.random.normal(ks[2], (d, d), dtype=jnp.float32) * s, 'bq': jnp.zeros((d,), jnp.float32), 'wk': jax.random.normal(ks[3], (d, d), dtype=jnp.float32) * s, 'bk': jnp.zeros((d,), jnp.float32), 'wv': jax.random.normal(ks[4], (d, d), dtype=jnp.float32) * s, 'bv': jnp.zeros((d,), jnp.float32), 'wo': jax.random.normal(ks[5], (d, d), dtype=jnp.float32) * s, 'bo': jnp.zeros((d,), jnp.float32), 'w1': jax.random.normal(ks[6], (d, f), dtype=jnp.float32) * s, 'b1': jnp.zeros((f,), jnp.float32), 'w2': jax.random.normal(ks[7], (f, d), dtype=jnp.float32) * (1.0 / np.sqrt(f)), 'b2': jnp.zeros((d,), jnp.float32), 'alpha1': jnp.ones((d,), jnp.float32), 'gamma1': jnp.ones((d,), jnp.float32), 'alpha2': jnp.ones((d,), jnp.float32), 'gamma2': jnp.ones((d,), jnp.float32)}
        return inp
    _L1_gnn_all = _L1_gnn_setup()
    _L1_gnn_in = {k: v for k, v in _L1_gnn_all.items() if k in ('wq', 'bq', 'wk', 'bk', 'wv', 'bv', 'wo', 'bo', 'w1', 'b1', 'w2', 'b2', 'alpha1', 'gamma1', 'alpha2', 'gamma2')}
    del _L1_gnn_all
    return {'x': x, 'adj': adj, 'L0_gnn_Wq': _L0_gnn_in['Wq'], 'L0_gnn_Wk': _L0_gnn_in['Wk'], 'L0_gnn_Wv': _L0_gnn_in['Wv'], 'L0_gnn_bv': _L0_gnn_in['bv'], 'L0_gnn_Wo': _L0_gnn_in['Wo'], 'L0_gnn_bo': _L0_gnn_in['bo'], 'L1_gnn_wq': _L1_gnn_in['wq'], 'L1_gnn_bq': _L1_gnn_in['bq'], 'L1_gnn_wk': _L1_gnn_in['wk'], 'L1_gnn_bk': _L1_gnn_in['bk'], 'L1_gnn_wv': _L1_gnn_in['wv'], 'L1_gnn_bv': _L1_gnn_in['bv'], 'L1_gnn_wo': _L1_gnn_in['wo'], 'L1_gnn_bo': _L1_gnn_in['bo'], 'L1_gnn_w1': _L1_gnn_in['w1'], 'L1_gnn_b1': _L1_gnn_in['b1'], 'L1_gnn_w2': _L1_gnn_in['w2'], 'L1_gnn_b2': _L1_gnn_in['b2'], 'L1_gnn_alpha1': _L1_gnn_in['alpha1'], 'L1_gnn_gamma1': _L1_gnn_in['gamma1'], 'L1_gnn_alpha2': _L1_gnn_in['alpha2'], 'L1_gnn_gamma2': _L1_gnn_in['gamma2']}

def reference(x, adj, L0_gnn_Wq, L0_gnn_Wk, L0_gnn_Wv, L0_gnn_bv, L0_gnn_Wo, L0_gnn_bo, L1_gnn_wq, L1_gnn_bq, L1_gnn_wk, L1_gnn_bk, L1_gnn_wv, L1_gnn_bv, L1_gnn_wo, L1_gnn_bo, L1_gnn_w1, L1_gnn_b1, L1_gnn_w2, L1_gnn_b2, L1_gnn_alpha1, L1_gnn_gamma1, L1_gnn_alpha2, L1_gnn_gamma2):
    import jax
    import jax.numpy as jnp

    def _L0_gnn_ref(x, encoding_bias, Wq, Wk, Wv, bv, Wo, bo):
        import jax, jax.numpy as jnp
        import numpy as np
        NUM_HEADS = 12
        HIDDEN = 384
        HEAD = HIDDEN // NUM_HEADS
        SCALE = HIDDEN ** (-0.5)
        B, N, _ = x.shape
        q = (x @ Wq.T).reshape(B, N, NUM_HEADS, HEAD)
        k = (x @ Wk.T).reshape(B, N, NUM_HEADS, HEAD)
        v = (x @ Wv.T + bv).reshape(B, N, NUM_HEADS, HEAD)
        a = jnp.einsum('bnhd,bmhd->bhnm', q, k) * SCALE + encoding_bias[:, None, :, :]
        pad_mask = jnp.all(a == 0, axis=-1)
        a = jnp.where(pad_mask[..., None], -jnp.inf, a)
        a = jax.nn.softmax(a, axis=-1)
        a = jnp.nan_to_num(a)
        o = jnp.einsum('bhnm,bmhd->bnhd', a, v).reshape(B, N, HIDDEN)
        return o @ Wo.T + bo

    def _L1_gnn_ref(x, attn_bias, wq, bq, wk, bk, wv, bv, wo, bo, w1, b1, w2, b2, alpha1, gamma1, alpha2, gamma2):
        import jax, jax.numpy as jnp
        import numpy as np
        D_MODEL = 384
        NHEADS = 8
        D_FF = 1536
        B, N = (8, 512)
        EPS = 1e-06

        def _rmsnorm(x, alpha, gamma):
            x = x * jax.lax.rsqrt(jnp.mean(x * x, axis=-1, keepdims=True) + EPS)
            return alpha * x + gamma
        b, n, d = x.shape
        h = NHEADS
        dh = d // h
        scaling = dh ** (-0.5)

        def split_heads(t):
            return t.reshape(b, n, h, dh).transpose(0, 2, 1, 3)
        q = split_heads(x @ wq + bq)
        k = split_heads(x @ wk + bk)
        v = split_heads(x @ wv + bv)
        scores = jnp.einsum('bhqd,bhkd->bhqk', q, k) * scaling
        scores = scores + attn_bias[:, None, :, :]
        attn = jax.nn.softmax(scores, axis=-1)
        ctx = jnp.einsum('bhij,bhjd->bhid', attn, v)
        ctx = ctx.transpose(0, 2, 1, 3).reshape(b, n, d)
        attn_out = ctx @ wo + bo
        x = _rmsnorm(x + attn_out, alpha1, gamma1)
        ff = jax.nn.silu(x @ w1 + b1) @ w2 + b2
        x = _rmsnorm(x + ff, alpha2, gamma2)
        return x
    x = _layernorm(x + _L0_gnn_ref(x, adj, L0_gnn_Wq, L0_gnn_Wk, L0_gnn_Wv, L0_gnn_bv, L0_gnn_Wo, L0_gnn_bo), axis=-1)
    x = _layernorm(x + _L1_gnn_ref(x, adj, L1_gnn_wq, L1_gnn_bq, L1_gnn_wk, L1_gnn_bk, L1_gnn_wv, L1_gnn_bv, L1_gnn_wo, L1_gnn_bo, L1_gnn_w1, L1_gnn_b1, L1_gnn_w2, L1_gnn_b2, L1_gnn_alpha1, L1_gnn_gamma1, L1_gnn_alpha2, L1_gnn_gamma2), axis=-1)
    return x

_drawn_inputs = setup_inputs


def setup_inputs(seed=0):
    import zlib

    import numpy as np

    out = dict(_drawn_inputs(seed))
    spreads = {'L1_gnn_bq': (0.0, 0.8),
     'L1_gnn_bk': (0.0, 0.8),
     'L1_gnn_bv': (0.0, 0.1),
     'L1_gnn_bo': (0.0, 0.1),
     'L1_gnn_b1': (0.0, 0.329),
     'L1_gnn_b2': (0.0, 0.1),
     'L1_gnn_alpha1': (1.0, 0.2),
     'L1_gnn_gamma1': (1.0, 0.2),
     'L1_gnn_alpha2': (1.0, 0.2),
     'L1_gnn_gamma2': (1.0, 0.2)}
    factors = {'L0_gnn_bv': 5.101, 'L0_gnn_bo': 5.889}
    for name, (base, spread) in spreads.items():
        noise = np.random.default_rng([zlib.crc32(name.encode()), seed]).standard_normal(out[name].shape)
        drawn = base * np.exp(spread * noise) if base else spread * noise
        out[name] = jnp.asarray(drawn.astype(out[name].dtype))
    for name, factor in factors.items():
        out[name] = (out[name] * factor).astype(out[name].dtype)
    return out
```

```python
from contextlib import ExitStack

import concourse.bass as bass
from concourse import mybir

F32 = mybir.dt.float32
F32R = mybir.dt.float32r
ALU = mybir.AluOpType
ACT = mybir.ActivationFunctionType
AX = mybir.AxisListType

P = 128
D = 384
DC = D // P
G = 4
TOK = G * P
HIGH, LOW = 0, 1
PARTS = [(HIGH, HIGH), (HIGH, LOW), (LOW, HIGH)]
LOWEST = -3.4028234663852886e38
LN_EPS = 1e-5
RMS_EPS = 1e-6


def at_least(eng, sem, value):
    if isinstance(value, int) and value <= 0:
        return
    eng.wait_ge(sem, value)


def at_least_apart(eng, sem, value, passed):
    if isinstance(value, int):
        at_least(eng, sem, value)
    else:
        eng.wait_ge(sem, value)
        eng.sem_inc(passed, 1)


def walk_tiles(eng, tiles, body):
    for p in range(2):
        body(p, 0, p)
    with eng.Fori(1, tiles // 2 - 1) as pair:
        for p in range(2):
            body(pair * 2 + p, pair, p)
    for p in range(2):
        body(tiles - 2 + p, tiles // 2 - 1, p)


def attention_pass(nc, tag, x_in, adj_in, wq_in, wk_in, wv_in, wo_in, bq_in, bk_in, bv_in, bo_in,
                   alpha_in, gamma_in, out, heads, masked):
    B = x_in.shape[0]
    TILES = B // G
    DH = D // heads
    SCALE = float(D if masked else DH) ** -0.5
    HB = 4
    NB = heads // HB
    DHP = 32 if DH == 32 else 64
    OC = heads * DHP // P
    HPC = P // DHP
    blocks = []
    for c in range(DC):
        for h in range(heads):
            r0, r1 = max(h * DH, c * P), min((h + 1) * DH, (c + 1) * P)
            if r0 < r1:
                blocks.append((c, h, r0 - c * P, r1 - r0))
    NBLK = len(blocks)
    runs = []
    for i, (c, h, _, _) in enumerate(blocks):
        if runs and runs[-1][0] == c and h // HB == runs[-1][3] // HB:
            runs[-1][2] += 1
        else:
            runs.append([c, i, 1, h])
    biased = bq_in is not None
    rms = alpha_in is not None

    X_USE, K_USE, Q_USE, V_USE, USES = 0, DC, 2 * DC, 3 * DC, 3 * DC + G
    HIGHS = 3 * DC

    with ExitStack() as ctx:
        def sb(name, shape, dt=F32):
            return ctx.enter_context(nc.sbuf_tensor(f"{tag}_{name}", shape, dt))

        def sem(name):
            return ctx.enter_context(nc.semaphore(f"{tag}_{name}"))

        ident = sb("ident", [P, P])
        w_qkv = [sb(f"w_{n}", [P, 2, DC, D], F32R) for n in "qkv"]
        w_o = sb("w_o", [P, 2, OC, D], F32R)
        bv_b = sb("bv_b", [P, D])
        bo_b = sb("bo_b", [P, D])
        if biased:
            bq_c = sb("bq_c", [P, DC])
            bqs_c = sb("bqs_c", [P, DC])
            bk_c = sb("bk_c", [P, DC])
        if rms:
            alpha_b = sb("alpha_b", [P, D])
            gamma_b = sb("gamma_b", [P, D])
        x_nat = sb("x_nat", [P, G, D])
        xb = sb("xb", [P, 2, G, D])
        adj = sb("adj", [P, 2, G, P])
        xT = sb("xT", [P, 2, DC, TOK], F32R)
        qT = sb("qT", [P, 2, 2, DC, TOK], F32R)
        kT = sb("kT", [P, 2, 2, DC, TOK], F32R)
        k_blk = sb("k_blk", [P, 2, 2, NBLK, P], F32R)
        v = sb("v", [P, 2, G, heads, DHP])
        scores = sb("scores", [P, heads, P])
        probs = sb("probs", [P, 2, heads, P])
        pT = sb("pT", [P, max(heads, OC * 3), P])
        oT = sb("oT", [P, 2, OC, P], F32R)
        y = sb("y", [P, 2, D])
        o_nat = sb("o_nat", [P, 2, D])
        row_max = sb("row_max", [P, 2, heads])
        neg_max = sb("neg_max", [P, 2, heads])
        row_abs = sb("row_abs", [P, 2, heads])
        row_sum = sb("row_sum", [P, 2, heads])
        inv_sum = sb("inv_sum", [P, 2, heads])
        weight = sb("weight", [P, 2, heads])
        stats = sb("stats", [P, 6])
        mean_var = sb("mean_var", [P, 2, 2])
        ms = sb("ms", [P, 4])
        minus_half = sb("minus_half", [P, 1])

        bank = ctx.enter_context(nc.psum_tensor(f"{tag}_bank", [P, 8, 512], F32))
        s_bank = bank[:, 0:NB, :]
        t_bank = bank[:, 3:5, :]
        j_bank = bank[:, 5:7, :]
        o_bank = bank[:, 7, :]

        w_loaded = [sem(f"w_loaded{i}") for i in range(4)]
        vectors_loaded = sem("vectors_loaded")
        bias_scaled = sem("bias_scaled")
        blk_zeroed = sem("blk_zeroed")
        zeroed = sem("zeroed")
        const_made = sem("const_made")
        w_high = sem("w_high")
        w_low = sem("w_low")
        x_loaded = sem("x_loaded")
        adj_loaded = [sem(f"adj_loaded{i}") for i in range(2)]
        k_blk_loaded = [sem(f"k_blk_loaded{i}") for i in range(2)]
        stored = [sem(f"stored{i}") for i in range(2)]
        j_ready = sem("j_ready")
        s_ready = sem("s_ready")
        t_ready = sem("t_ready")
        pv_ready = sem("pv_ready")
        op_ready = sem("op_ready")
        high_done = sem("high_done")
        exp_done = sem("exp_done")
        pT_ready = sem("pT_ready")
        o_high_done = sem("o_high_done")
        j_done = sem("j_done")
        s_read = sem("s_read")
        neg_max_ready = sem("neg_max_ready")
        abs_done = sem("abs_done")
        inv_ready = sem("inv_ready")
        weight_ready = sem("weight_ready")
        o_low_done = sem("o_low_done")
        y_ready = sem("y_ready")
        stats_ready = sem("stats_ready")
        mean_var_ready = sem("mean_var_ready")
        xb_ready = sem("xb_ready")
        probs_ready = sem("probs_ready")
        pool_step = sem("pool_step")
        fin_ready = sem("fin_ready")
        dve_passed, pool_passed, sp_passed = sem("dve_passed"), sem("pool_passed"), sem("sp_passed")

        x_v = x_in.rearrange("(t g) p d -> t p g d", g=G)
        adj_v = adj_in.rearrange("(t g) p k -> t p g k", g=G)
        out_v = out.rearrange("(t g) p d -> t g p d", g=G)

        stage = [xb[:, 0, :, :].rearrange("p g d -> p (g d)")[:, 0:DC * D].rearrange("p (c d) -> p c d", c=DC),
                 xb[:, 1, :, :].rearrange("p g d -> p (g d)")[:, 0:DC * D].rearrange("p (c d) -> p c d", c=DC),
                 v[:, :, :, :, :].rearrange("p a g h d -> p (a g h d)")[:, 0:DC * D].rearrange("p (c d) -> p c d", c=DC),
                 pT[:, :, :].rearrange("p h k -> p (h k)")[:, 0:OC * D].rearrange("p (c d) -> p c d", c=OC)]

        FIRST = [("X", 0), ("X", 1), ("X", 2), ("K", 0), ("K", 1), ("K", 2),
                 ("Q", 0), ("Q", 1), ("Q", 2), ("V", 0), ("V", 1), ("V", 2), ("V", 3)]
        EARLY = [[("X", 0), ("X", 1)], [], [], []]
        BEFORE = [[("X", 2)], [("K", 2), ("Q", 0)], [("Q", 2), ("V", 0)], [("V", 2)]]
        AFTER = [[("K", 0), ("K", 1)], [("Q", 1)], [("V", 1)], [("V", 3)]]
        EXPS = [{("X", 1): 4, "pT": 8, ("K", 0): 12}, {"start": 5, ("K", 2): 9, "pT": 12},
                {"start": 5, ("Q", 2): 8, "pT": 12}, {"start": 4, "pT": 12}]
        USE = {"X": X_USE, "K": K_USE, "Q": Q_USE, "V": V_USE}
        is_last = lambda t: isinstance(t, int) and t == TILES - 1

        block = ctx.enter_context(nc.Block())

        weights = [(stage[0], wk_in, w_qkv[1], 1.0), (stage[1], wq_in, w_qkv[0], SCALE),
                   (stage[2], wv_in, w_qkv[2], 1.0), (stage[3], wo_in, w_o, 1.0)]
        W_READY = {"K": 1, "Q": 2, "V": 3, "O": 4}
        vectors = [(bv_b, bv_in), (bo_b, bo_in)] + ([(alpha_b, alpha_in), (gamma_b, gamma_in)] if rms else [])
        columns = [(bq_c, bq_in), (bk_c, bk_in)] if biased else []
        n_vectors = len(vectors) + len(columns)
        n_wo = 1 if DHP == DH else heads

        @block.sync
        def _(sp):
            def load_w(i):
                st, w, _, _ = weights[i]
                sp.dma_start(st, w.rearrange("(c p) n -> p c n", p=P)).then_inc(w_loaded[i], 16)

            def load_x(t):
                sp.dma_start(x_nat[:, :, :], x_v[bass.ds(t, 1)].rearrange("a p g d -> p (a g) d")).then_inc(x_loaded, 16)

            def load_adj(t, p):
                sp.dma_start(adj[:, p, :, :], adj_v[bass.ds(t, 1)].rearrange("a p g d -> p (a g) d")).then_inc(adj_loaded[p], 16)

            def load_k_blk(t, p, g):
                n = t * G + g
                at_least_apart(sp, high_done, t * HIGHS + 2 * DC, sp_passed)
                at_least_apart(sp, j_done, t * USES + Q_USE, sp_passed)
                at_least_apart(sp, s_ready, (n - 1) * NB, sp_passed)
                if DH == 32:
                    for j in range(HB):
                        r = j * DH
                        sp.dma_start(
                            k_blk[r:r + DH, g % 2, :, :, :].rearrange("p s (c j) k -> p (s c) j k", j=HB)[:, :, j, :].bitcast(F32),
                            kT[r:r + DH, p, :, :, g * P:(g + 1) * P].rearrange("p s c k -> p (s c) k").bitcast(F32),
                        ).then_inc(k_blk_loaded[g % 2], 16)
                else:
                    for i, (c, _, r, rows) in enumerate(blocks):
                        sp.dma_start(k_blk[r:r + rows, g % 2, :, i, :].bitcast(F32),
                                     kT[r:r + rows, p, :, c, g * P:(g + 1) * P].bitcast(F32)).then_inc(k_blk_loaded[g % 2], 16)

            def store(t, g):
                n = t * G + g
                at_least_apart(sp, fin_ready, n + 1, sp_passed)
                sp.dma_start(out_v[bass.ds(t, 1), g].rearrange("a p d -> p (a d)"), o_nat[:, g % 2, :]).then_inc(stored[g % 2], 16)

            load_x(0)
            load_w(0)
            load_w(1)
            for dst, src in columns:
                with nc.allow_non_contiguous_dma(reason="bias columns, 384 elements once"):
                    sp.dma_start(dst[:, :], src.rearrange("(c p) -> p c", p=P)).then_inc(vectors_loaded, 16)
            for dst, src in vectors:
                sp.dma_start(dst[:, :], src.rearrange("(a d) -> a d", a=1).to_broadcast([P, D])).then_inc(vectors_loaded, 16)
            load_w(2)
            load_adj(0, 0)
            load_adj(1, 1)
            if DHP == DH:
                load_w(3)
            else:
                sp.wait_ge(zeroed, 2)
                for h in range(heads):
                    r = (h % HPC) * DHP
                    sp.dma_start(stage[3][r:r + DH, h // HPC, :], wo_in[h * DH:(h + 1) * DH, :]).then_inc(w_loaded[3], 16)
            sp.wait_ge(j_ready, DC)
            sp.wait_ge(xb_ready, 1)
            load_x(1)
            sp.wait_ge(blk_zeroed, 1)
            load_k_blk(0, 0, 0)
            sp.wait_ge(blk_zeroed, 2)
            load_k_blk(0, 0, 1)

            def tile(t, pair, p):
                for g in range(G):
                    if not (is_last(t) and g >= 2):
                        load_k_blk(t + (g + 2) // G, (p + (g + 2) // G) % 2, (g + 2) % G)
                    more = not (isinstance(t, int) and t >= TILES - 2)
                    if g == 1 and more:
                        at_least_apart(sp, j_ready, (t + 1) * USES + DC, sp_passed)
                        at_least_apart(sp, xb_ready, t + 2, sp_passed)
                        load_x(t + 2)
                    if g == 3 and more:
                        at_least_apart(sp, s_read, (t * G + G) * NB, sp_passed)
                        load_adj(t + 2, p)
                    if g >= 2:
                        store(t, g - 2)
                    elif not (isinstance(t, int) and t == 0):
                        store(t - 1, g + 2)

            walk_tiles(sp, TILES, tile)
            store(TILES - 1, 2)
            store(TILES - 1, 3)
            for i in range(2):
                sp.wait_ge(stored[i], 16 * B // 2)

        @block.tensor
        def _(pe):
            def free_j(u):
                at_least(pe, j_done, u - 1)

            def project(t, p, kind, i):
                u = t * USES + USE[kind] + i
                dst = j_bank[:, (p + USE[kind] + i) % 2, :]
                if kind == "X":
                    if i == 0:
                        at_least(pe, x_loaded, 16 * (t + 1))
                    free_j(u)
                    for g in range(G):
                        mm = pe.transpose(dst[:, g * P:(g + 1) * P], x_nat[:, g, i * P:(i + 1) * P], ident[:, :])
                elif kind in "QK":
                    at_least(pe, j_done, t * USES + DC)
                    free_j(u)
                    w = w_qkv["QK".index(kind)]
                    todo = [(c, a, b) for c in range(DC) for a, b in PARTS]
                    for k, (c, a, b) in enumerate(todo):
                        mm = pe.matmul(dst, w[:, a, c, i * P:(i + 1) * P], xT[:, b, c, :],
                                       start=k == 0, stop=k == len(todo) - 1)
                else:
                    at_least(pe, j_done, t * USES + DC)
                    free_j(u)
                    todo = [(c, a, b) for c in range(DC) for a, b in PARTS]
                    for k, (c, a, b) in enumerate(todo):
                        mm = pe.matmul(dst[:, 0:D], xT[:, a, c, i * P:(i + 1) * P], w_qkv[2][:, b, c, :],
                                       start=k == 0, stop=k == len(todo) - 1)
                mm.then_inc(j_ready, 1)

            def score(t, p, g):
                n = t * G + g
                at_least(pe, k_blk_loaded[g % 2], 16 * (HB if DH == 32 else NBLK) * (t * 2 + g // 2 + 1))
                at_least(pe, j_done, t * USES + V_USE)
                for b in range(NB):
                    mine = [r for r in runs if r[3] // HB == b]
                    at_least(pe, s_read, (n - 1) * NB + b + 1)
                    for k, (c, i, m, h) in enumerate(mine):
                        for a, part in enumerate(PARTS):
                            col = (h % HB) * P
                            mm = pe.matmul(s_bank[:, b, col:col + m * P], qT[:, p, part[0], c, g * P:(g + 1) * P],
                                           k_blk[:, g % 2, part[1], i:i + m, :],
                                           start=k == 0 and a == 0, stop=k == len(mine) - 1 and a == 2,
                                           skip_group_check=len(mine) > 1)
                    mm.then_inc(s_ready, 1)

            def turn(t, g):
                n = t * G + g
                for q in range(NB):
                    at_least(pe, probs_ready, n * NB + q + 1)
                    at_least(pe, pT_ready, n * NB + q - 1)
                    for j in range(HB):
                        mm = pe.transpose(t_bank[:, (NB * g + q) % 2, j * P:(j + 1) * P],
                                          probs[:, g % 2, q * HB + j, :], ident[:, :])
                    mm.then_inc(t_ready, 1)

            def attend(t, p, g):
                n = t * G + g
                at_least(pe, j_done, t * USES + V_USE + g + 1)
                at_least(pe, y_ready, n)
                for h in range(heads):
                    if h % HB == 0:
                        at_least(pe, pT_ready, n * NB + h // HB + 1)
                    r = (h % HPC) * DHP
                    c = h // HPC
                    mm = pe.matmul(o_bank[r:r + DHP, c * P:(c + 1) * P], v[:, p, g, h, :], pT[:, h, :],
                                   start=True, stop=True)
                mm.then_inc(pv_ready, 1)

            def output(t, g):
                n = t * G + g
                at_least(pe, o_low_done, n + 1)
                todo = [(c, a, b) for c in range(OC) for a, b in PARTS]
                for k, (c, a, b) in enumerate(todo):
                    mm = pe.matmul(o_bank[:, 0:D], oT[:, a, c, :], w_o[:, b, c, :],
                                   start=k == 0, stop=k == len(todo) - 1)
                mm.then_inc(op_ready, 1)

            pe.wait_ge(const_made, 2)
            for kind, i in FIRST:
                if kind != "X" and i == 0:
                    pe.wait_ge(w_low, W_READY[kind])
                project(0, 0, kind, i)
            score(0, 0, 0)
            pe.wait_ge(w_low, W_READY["O"])

            def tile(t, pair, p):
                for g in range(G):
                    last = is_last(t)
                    if g < G - 1:
                        score(t, p, g + 1)
                    elif not last:
                        score(t + 1, 1 - p, 0)
                    if not last:
                        for kind, i in EARLY[g]:
                            project(t + 1, 1 - p, kind, i)
                    if g > 0:
                        output(t, g - 1)
                    elif not (isinstance(t, int) and t == 0):
                        output(t - 1, G - 1)
                    if not last:
                        for kind, i in BEFORE[g]:
                            project(t + 1, 1 - p, kind, i)
                    turn(t, g)
                    if not last:
                        for kind, i in AFTER[g]:
                            project(t + 1, 1 - p, kind, i)
                    attend(t, p, g)

            walk_tiles(pe, TILES, tile)
            output(TILES - 1, G - 1)

        @block.scalar
        def _(act):
            def high_w(i):
                st, _, dst, scale = weights[i]
                act.wait_ge(w_loaded[i], 16 * (n_wo if i == 3 else 1))
                act.activation(dst[:, HIGH, :, :], st, ACT.Copy, scale=scale).then_inc(w_high, 1)

            def high(t, p, kind, i):
                at_least(act, j_ready, t * USES + USE[kind] + i + 1)
                src = j_bank[:, (p + USE[kind] + i) % 2, :]
                if kind == "X":
                    op = act.activation(xT[:, HIGH, i, :], src, ACT.Copy)
                else:
                    dst = (qT if kind == "Q" else kT)[:, p, HIGH, i, :]
                    if biased:
                        op = act.activation(dst, src, ACT.Identity, bias=(bqs_c if kind == "Q" else bk_c)[:, i:i + 1])
                    else:
                        op = act.activation(dst, src, ACT.Copy)
                op.then_inc(high_done, 1)

            def exp(t, g, h):
                n = t * G + g
                if h == 0:
                    at_least(act, neg_max_ready, n + 1)
                    at_least(act, t_ready, (n - 1) * NB)
                op = act.activation(probs[:, g % 2, h, :], scores[:, h, :], ACT.Exp,
                                    bias=neg_max[:, g % 2, h:h + 1], accum_out=row_sum[:, g % 2, h:h + 1])
                if h % HB == HB - 1:
                    op.then_inc(exp_done, 1)

            def copy_pT(t, g, q):
                n = t * G + g
                at_least(act, t_ready, n * NB + q + 1)
                act.activation(pT[:, q * HB:(q + 1) * HB, :].rearrange("p h k -> p (h k)"),
                               t_bank[:, (NB * g + q) % 2, :], ACT.Copy).then_inc(pT_ready, 1)

            def high_o(t, g):
                at_least(act, pv_ready, t * G + g + 1)
                act.activation(oT[:, HIGH, :, :].rearrange("p c k -> p (c k)"), o_bank[:, 0:OC * P],
                               ACT.Copy).then_inc(o_high_done, 1)

            for kind, i in FIRST:
                if kind == "X":
                    high(0, 0, kind, i)
            high_w(0)
            high_w(1)
            if biased:
                act.wait_ge(vectors_loaded, 16 * n_vectors)
                act.activation(bqs_c[:, :], bq_c[:, :], ACT.Copy, scale=SCALE).then_inc(bias_scaled, 1)
                act.wait_ge(bias_scaled, 1)
            for kind, i in FIRST:
                if kind in "KQ":
                    high(0, 0, kind, i)
                if (kind, i) == ("K", 0):
                    high_w(2)
            high_w(3)
            for h in range(heads):
                exp(0, 0, h)

            def tile(t, pair, p):
                for g in range(G):
                    last = is_last(t)
                    nt, ng = (t, g + 1) if g < G - 1 else (t + 1, 0)
                    done = 0

                    def exps(mark):
                        nonlocal done
                        if not (last and g == G - 1):
                            upto = heads * EXPS[g].get(mark, 0) // 12
                            for h in range(done, upto):
                                exp(nt, ng, h)
                            done = max(done, upto)

                    def highs(uses):
                        for kind, i in uses:
                            if kind != "V" and not last:
                                high(t + 1, 1 - p, kind, i)
                            exps((kind, i))

                    exps("start")
                    highs(EARLY[g] + BEFORE[g])
                    for q in range(NB):
                        copy_pT(t, g, q)
                    exps("pT")
                    highs(AFTER[g])
                    high_o(t, g)

            walk_tiles(act, TILES, tile)

        @block.vector
        def _(dve):
            dve.memset(minus_half[:, :], -0.5).then_inc(zeroed, 1)
            if DHP != DH:
                dve.memset(stage[3], 0.0).then_inc(zeroed, 1)

            def low_w(i):
                st, _, dst, scale = weights[i]
                dve.wait_ge(w_high, i + 1)
                dve.scalar_tensor_tensor(out=dst[:, LOW, :, :], in0=st, scalar=scale,
                                         in1=dst[:, HIGH, :, :].bitcast(F32), op0=ALU.mult,
                                         op1=ALU.subtract).then_inc(w_low, 1)

            def evacuate(t, p, kind, i):
                u = t * USES + USE[kind] + i
                src = j_bank[:, (p + USE[kind] + i) % 2, :]
                if kind == "V":
                    at_least(dve, j_ready, u + 1)
                    op = dve.tensor_tensor(v[:, p, i, :, 0:DH], src[:, 0:D].rearrange("p (h d) -> p h d", h=heads),
                                           bv_b[:, :].rearrange("p (h d) -> p h d", h=heads), ALU.add)
                else:
                    at_least(dve, high_done, t * HIGHS + USE[kind] + i + 1)
                    if kind == "X":
                        dst, hi = xT[:, LOW, i, :], xT[:, HIGH, i, :]
                    else:
                        k = qT if kind == "Q" else kT
                        dst, hi = k[:, p, LOW, i, :], k[:, p, HIGH, i, :]
                    if biased and kind != "X":
                        op = dve.scalar_tensor_tensor(out=dst, in0=src, scalar=(bqs_c if kind == "Q" else bk_c)[:, i:i + 1],
                                                      in1=hi.bitcast(F32), op0=ALU.add, op1=ALU.subtract)
                    else:
                        op = dve.tensor_tensor(dst, src, hi.bitcast(F32), ALU.subtract)
                op.then_inc(j_done, 1)

            def add_adjacency(t, pair, p, g):
                n = t * G + g
                if g == 0:
                    at_least(dve, adj_loaded[p], 16 * (pair + 1))
                at_least(dve, exp_done, n * NB)
                if masked:
                    at_least(dve, abs_done, n)
                for h in range(heads):
                    if h % HB == 0:
                        at_least_apart(dve, s_ready, n * NB + h // HB + 1, dve_passed)
                    op = dve.tensor_tensor_reduce(out=scores[:, h, :], in0=s_bank[:, h // HB, (h % HB) * P:(h % HB + 1) * P],
                                                  in1=adj[:, p, g, :], scale=1.0, scalar=LOWEST, op0=ALU.add,
                                                  op1=ALU.max, accum_out=row_max[:, g % 2, h:h + 1])
                    if h % HB == HB - 1:
                        op.then_inc(s_read, 1)
                at_least(dve, s_read, (n + 1) * NB)
                dve.tensor_scalar(neg_max[:, g % 2, :], row_max[:, g % 2, :], -1.0, None,
                                  ALU.mult).then_inc(neg_max_ready, 1)

            def largest(t, g):
                dve.tensor_reduce(row_abs[:, g % 2, :], scores[:, :, :], AX.X, ALU.max,
                                  apply_absolute_value=True).then_inc(abs_done, 1)

            def weigh(t, g):
                n = t * G + g
                at_least(dve, exp_done, (n + 1) * NB)
                dst = inv_sum if masked else weight
                dve.reciprocal(dst[:, g % 2, :], row_sum[:, g % 2, :]).then_inc(inv_ready if masked else weight_ready, 1)
                if masked:
                    at_least(dve, inv_ready, n + 1)
                    at_least(dve, abs_done, n + 1)
                    dve.scalar_tensor_tensor(out=weight[:, g % 2, :], in0=row_abs[:, g % 2, :], scalar=0.0,
                                             in1=inv_sum[:, g % 2, :], op0=ALU.is_gt,
                                             op1=ALU.mult).then_inc(weight_ready, 1)

            def residual(t, p, g):
                n = t * G + g
                at_least(dve, op_ready, n + 1)
                at_least(dve, xb_ready, t + 1)
                at_least(dve, fin_ready, n - 1)
                dve.tensor_tensor(y[:, g % 2, :], o_bank[:, 0:D], xb[:, p, g, :], ALU.add).then_inc(y_ready, 1)

            def moments(t, g):
                n = t * G + g
                at_least(dve, y_ready, n + 1)
                dve.bn_stats(stats[:, :], y[:, g % 2, :]).then_inc(stats_ready, 1)
                at_least_apart(dve, stats_ready, n + 1, dve_passed)
                dve.bn_aggr(mean_var[:, g % 2, :], stats[:, :]).then_inc(mean_var_ready, 1)

            def low_o(t, g):
                at_least(dve, o_high_done, t * G + g + 1)
                dve.tensor_tensor(oT[:, LOW, :, :].rearrange("p c k -> p (c k)"), o_bank[:, 0:OC * P],
                                  oT[:, HIGH, :, :].rearrange("p c k -> p (c k)").bitcast(F32),
                                  ALU.subtract).then_inc(o_low_done, 1)

            for kind, i in FIRST:
                if (kind, i) == ("K", 0):
                    low_w(0)
                    low_w(1)
                    dve.wait_ge(vectors_loaded, 16 * n_vectors)
                    if biased:
                        dve.wait_ge(bias_scaled, 1)
                if (kind, i) == ("K", 1):
                    low_w(2)
                    if DHP != DH:
                        dve.wait_ge(w_low, 3)
                        dve.memset(v[:, :, :, :, DH:DHP].rearrange("p a g h d -> p (a g h) d"), 0.0).then_inc(zeroed, 1)
                evacuate(0, 0, kind, i)
            low_w(3)
            add_adjacency(0, 0, 0, 0)
            if masked:
                largest(0, 0)
            weigh(0, 0)

            def tile(t, pair, p):
                for g in range(G):
                    last = is_last(t)
                    final = last and g == G - 1
                    nt, npair, np_, ng = (t, pair, p, g + 1) if g < G - 1 else (t + 1, pair + p, 1 - p, 0)
                    if not final:
                        add_adjacency(nt, npair, np_, ng)
                    if not last:
                        for kind, i in EARLY[g]:
                            evacuate(t + 1, 1 - p, kind, i)
                    if g > 0:
                        residual(t, p, g - 1)
                        moments(t, g - 1)
                    elif not (isinstance(t, int) and t == 0):
                        residual(t - 1, 1 - p, G - 1)
                    if not last:
                        for kind, i in BEFORE[g]:
                            evacuate(t + 1, 1 - p, kind, i)
                    if g == 0 and not (isinstance(t, int) and t == 0):
                        moments(t - 1, G - 1)
                    if masked and not final:
                        largest(nt, ng)
                    if not last:
                        for kind, i in AFTER[g]:
                            evacuate(t + 1, 1 - p, kind, i)
                    if not final:
                        weigh(nt, ng)
                    low_o(t, g)

            walk_tiles(dve, TILES, tile)
            residual(TILES - 1, 1, G - 1)
            moments(TILES - 1, G - 1)

        @block.gpsimd
        def _(pool):
            pool.memset(ident[:, :], 0.0).then_inc(const_made, 1)
            pool.wait_ge(const_made, 1)
            pool.affine_select(out=ident[:, :], in_=ident[:, :], compare_op=ALU.not_equal, fill=1.0,
                               base=0, pattern=[[-1, P]], channel_multiplier=1).then_inc(const_made, 1)
            for i in range(2):
                pool.memset(k_blk[:, i, :, :, :].rearrange("p s b k -> p (s b k)").bitcast(F32), 0.0).then_inc(blk_zeroed, 1)
            pool.wait_ge(w_low, 2)
            pool.wait_ge(zeroed, 1)
            pool.wait_ge(vectors_loaded, 16 * n_vectors)

            STEPS = 5 if rms else 3

            def add_bo(t, p):
                at_least(pool, x_loaded, 16 * (t + 1))
                at_least(pool, y_ready, G * (t - 1))
                pool.tensor_tensor(xb[:, p, :, :], x_nat[:, :, :],
                                   bo_b[:, :].unsqueeze(1).to_broadcast([P, G, D]), ALU.add).then_inc(xb_ready, 1)

            def normalise(t, g):
                n = t * G + g
                at_least(pool, weight_ready, n + 1)
                for q in range(NB):
                    hs = slice(q * HB, (q + 1) * HB)
                    pool.tensor_tensor(probs[:, g % 2, hs, :], probs[:, g % 2, hs, :],
                                       weight[:, g % 2, hs].unsqueeze(2).to_broadcast([P, HB, P]),
                                       ALU.mult).then_inc(probs_ready, 1)

            def finish(t, g):
                n = t * G + g
                at_least(pool, mean_var_ready, n + 1)
                at_least_apart(pool, stored[g % 2], 16 * (t * 2 + g // 2), pool_passed)
                mean, var = mean_var[:, g % 2, 0:1], mean_var[:, g % 2, 1:2]
                done = n * STEPS
                if rms:
                    pool.tensor_tensor(ms[:, 0:1], mean, mean, ALU.mult).then_inc(pool_step, 1)
                    at_least_apart(pool, pool_step, done + 1, pool_passed)
                    pool.tensor_scalar(ms[:, 1:2], ms[:, 0:1], var, RMS_EPS, ALU.add, ALU.add).then_inc(pool_step, 1)
                    done = done + 1
                else:
                    pool.tensor_scalar(ms[:, 1:2], var, LN_EPS, None, ALU.add).then_inc(pool_step, 1)
                pool.wait_ge(pool_step, done + 1)
                pool.tensor_tensor(ms[:, 2:3], ms[:, 1:2], minus_half[:, :], ALU.pow).then_inc(pool_step, 1)
                at_least_apart(pool, pool_step, done + 2, pool_passed)
                if rms:
                    pool.tensor_tensor(o_nat[:, g % 2, :], y[:, g % 2, :], alpha_b[:, :], ALU.mult).then_inc(pool_step, 1)
                    at_least_apart(pool, pool_step, done + 3, pool_passed)
                    pool.tensor_scalar(o_nat[:, g % 2, :], o_nat[:, g % 2, :], ms[:, 2:3], 1.0,
                                       ALU.mult, ALU.mult).then_inc(pool_step, 1)
                    at_least_apart(pool, pool_step, done + 4, pool_passed)
                    pool.tensor_tensor(o_nat[:, g % 2, :], o_nat[:, g % 2, :], gamma_b[:, :], ALU.add).then_inc(fin_ready, 1)
                else:
                    pool.tensor_scalar(ms[:, 3:4], mean, ms[:, 2:3], -1.0, ALU.mult, ALU.mult).then_inc(pool_step, 1)
                    at_least_apart(pool, pool_step, done + 3, pool_passed)
                    pool.tensor_scalar(o_nat[:, g % 2, :], y[:, g % 2, :], ms[:, 2:3], ms[:, 3:4],
                                       ALU.mult, ALU.add).then_inc(fin_ready, 1)

            add_bo(0, 0)
            normalise(0, 0)

            def tile(t, pair, p):
                for g in range(G):
                    if g == 0 and not is_last(t):
                        add_bo(t + 1, 1 - p)
                    if g > 0:
                        finish(t, g - 1)
                    elif not (isinstance(t, int) and t == 0):
                        finish(t - 1, G - 1)
                    if g < G - 1:
                        normalise(t, g + 1)
                    elif not is_last(t):
                        normalise(t + 1, 0)

            walk_tiles(pool, TILES, tile)
            finish(TILES - 1, G - 1)


def feed_forward_pass(nc, x_in, h_in, w1_in, b1_in, w2_in, b2_in, alpha_in, gamma_in, out):
    TILES = x_in.shape[0] // G
    FF = w1_in.shape[1]
    FC = FF // P
    LAG = 2
    TURN = 6
    RING = 3
    with ExitStack() as ctx:
        def sb(name, shape, dt=F32):
            return ctx.enter_context(nc.sbuf_tensor(f"ff_{name}", shape, dt))

        def sem(name):
            return ctx.enter_context(nc.semaphore(f"ff_{name}"))

        ident = sb("ident", [P, P])
        w1 = sb("w1", [P, 2, DC, FF], F32R)
        w2 = sb("w2", [P, 2, FC, D], F32R)
        b1_c = sb("b1_c", [P, FC])
        b2_b = sb("b2_b", [P, D])
        alpha_b = sb("alpha_b", [P, D])
        gamma_b = sb("gamma_b", [P, D])
        h_nat = sb("h_nat", [P, G, D])
        x_nat = sb("x_nat", [P, G, D])
        hb = sb("hb", [P, 2, G, D])
        xg = sb("xg", [P, 2, G, D])
        hT = sb("hT", [P, 2, 2, DC, TOK], F32R)
        act_out = sb("act_out", [P, 2, TOK])
        gT = sb("gT", [P, RING, 2, TOK], F32R)
        y = sb("y", [P, G, D])
        z = sb("z", [P, G, D])
        o_nat = sb("o_nat", [P, G, D])
        stats = sb("stats", [P, 2, G, 6])
        mean_var = sb("mean_var", [P, 2, G, 2])
        ms = sb("ms", [P, 6, G])
        minus_half = sb("minus_half", [P, G])

        bank = ctx.enter_context(nc.psum_tensor("ff_bank", [P, 8, 512], F32))
        f_bank = bank[:, 0:2, :]
        x_bank = bank[:, 2:4, :]
        y_bank = bank[:, 4:8, :]

        w_loaded = sem("w_loaded")
        const_made = sem("const_made")
        w_high = sem("w_high")
        w_low = sem("w_low")
        h_loaded = sem("h_loaded")
        x_loaded = sem("x_loaded")
        stored = sem("stored")
        hT_psum = sem("hT_psum")
        f_ready = sem("f_ready")
        f2_done = sem("f2_done")
        y_psum = sem("y_psum")
        hT_high = sem("hT_high")
        hT_low = sem("hT_low")
        silu_done = sem("silu_done")
        g_high = sem("g_high")
        g_low = sem("g_low")
        y_ready = sem("y_ready")
        y_stats = sem("y_stats")
        y_moments = sem("y_moments")
        y_scaled = sem("y_scaled")
        z_ready = sem("z_ready")
        z_stats = sem("z_stats")
        z_moments = sem("z_moments")
        sums_ready = sem("sums_ready")
        pool_step = sem("pool_step")
        rms_ready = sem("rms_ready")
        shift_ready = sem("shift_ready")
        fin_ready = sem("fin_ready")
        dve_passed, pool_passed, sp_passed = sem("dve_passed"), sem("pool_passed"), sem("sp_passed")

        x_v = x_in.rearrange("(t g) p d -> t p g d", g=G)
        h_v = h_in.rearrange("(t g) p d -> t p g d", g=G)
        out_v = out.rearrange("(t g) p d -> t p g d", g=G)
        stage1 = hb[:, :, :, :].rearrange("p a g d -> p (a g d)")
        stage2 = xg[:, :, :, :].rearrange("p a g d -> p (a g d)")
        block = ctx.enter_context(nc.Block())
        is_last = lambda t: isinstance(t, int) and t == TILES - 1
        w1_v = w1_in.rearrange("(c p) n -> p c n", p=P)
        w2_v = w2_in.rearrange("(c p) n -> p c n", p=P)
        S1 = stage1[:, 0:2 * FF]
        S2 = stage2[:, 0:2 * FF]
        CD = 2 * FF // D
        pieces = [
            (S1.rearrange("p (c n) -> p c n", c=2), w1[:, :, 0:2, :], w1_v[:, 0:2, :]),
            (S2[:, 0:FF].rearrange("p (c n) -> p c n", c=1), w1[:, :, 2:3, :], w1_v[:, 2:3, :]),
            (S1.rearrange("p (c n) -> p c n", c=CD), w2[:, :, 0:CD, :], w2_v[:, 0:CD, :]),
            (S2[:, 0:FF].rearrange("p (c n) -> p c n", n=D), w2[:, :, CD:FC, :], w2_v[:, CD:FC, :]),
        ]
        vectors = [(b2_b, b2_in), (alpha_b, alpha_in), (gamma_b, gamma_in)]

        @block.sync
        def _(sp):
            for dst, src in vectors:
                sp.dma_start(dst[:, :], src.rearrange("(a d) -> a d", a=1).to_broadcast([P, D])).then_inc(w_loaded, 16)
            with nc.allow_non_contiguous_dma(reason="bias column, 1536 elements once"):
                sp.dma_start(b1_c[:, :], b1_in.rearrange("(c p) -> p c", p=P)).then_inc(w_loaded, 16)
            sp.wait_ge(w_loaded, 16 * 4)
            for i, (st, _, src) in enumerate(pieces):
                at_least_apart(sp, w_low, i - 1, sp_passed)
                sp.dma_start(st, src).then_inc(w_loaded, 16)
                sp.wait_ge(w_loaded, 16 * (5 + i))

            def load(t):
                sp.dma_start(h_nat[:, :, :], h_v[bass.ds(t, 1)].rearrange("a p g d -> p (a g) d")).then_inc(h_loaded, 16)
                sp.dma_start(x_nat[:, :, :], x_v[bass.ds(t, 1)].rearrange("a p g d -> p (a g) d")).then_inc(x_loaded, 16)

            load(0)

            def tile(t, pair, p):
                if not is_last(t):
                    at_least_apart(sp, hT_psum, (t + 1) * DC, sp_passed)
                    at_least_apart(sp, sums_ready, 2 * (t + 1), sp_passed)
                    load(t + 1)
                if not (isinstance(t, int) and t == 0):
                    at_least_apart(sp, fin_ready, t * G, sp_passed)
                    sp.dma_start(out_v[bass.ds(t - 1, 1)].rearrange("a p g d -> p (a g) d"), o_nat[:, :, :]).then_inc(stored, 16)

            walk_tiles(sp, TILES, tile)
            sp.wait_ge(fin_ready, TILES * G)
            sp.dma_start(out_v[TILES - 1], o_nat[:, :, :]).then_inc(stored, 16)
            sp.wait_ge(stored, 16 * TILES)

        @block.tensor
        def _(pe):
            def turn(t, p, c):
                if c == 0:
                    at_least(pe, h_loaded, 16 * (t + 1))
                at_least(pe, hT_low, t * DC + c - 1)
                for g in range(G):
                    mm = pe.transpose(x_bank[:, (p + c) % 2, g * P:(g + 1) * P], h_nat[:, g, c * P:(c + 1) * P], ident[:, :])
                mm.then_inc(hT_psum, 1)

            def first(t, p, m):
                if m == 0:
                    at_least(pe, hT_low, (t + 1) * DC)
                at_least(pe, silu_done, t * FC + m - 1)
                todo = [(c, a, b) for c in range(DC) for a, b in PARTS]
                for k, (c, a, b) in enumerate(todo):
                    mm = pe.matmul(f_bank[:, m % 2, :], w1[:, a, c, m * P:(m + 1) * P], hT[:, p, b, c, :],
                                   start=k == 0, stop=k == len(todo) - 1)
                mm.then_inc(f_ready, 1)

            def second(t, m):
                at_least(pe, g_low, t * FC + m + 1)
                for g in range(G):
                    if m == 0:
                        at_least(pe, y_ready, (t - 1) * G + g + 1)
                    for k, (a, b) in enumerate(PARTS):
                        mm = pe.matmul(y_bank[:, g, 0:D], gT[:, m % RING, a, g * P:(g + 1) * P], w2[:, b, m, :],
                                       start=m == 0 and k == 0, stop=m == FC - 1 and k == 2)
                    if m == FC - 1 and g < G - 1:
                        mm.then_inc(y_psum, 1)
                if m == FC - 1:
                    mm.then_inc(y_psum, 1)
                else:
                    mm.then_inc(f2_done, 1)

            pe.wait_ge(const_made, 2)
            for c in range(DC):
                turn(0, 0, c)
            pe.wait_ge(w_low, 4)

            def tile(t, pair, p):
                for m in range(FC):
                    first(t, p, m)
                    if m >= LAG:
                        second(t, m - LAG)
                    elif not (isinstance(t, int) and t == 0):
                        second(t - 1, FC + m - LAG)
                    if TURN <= m < TURN + DC and not is_last(t):
                        turn(t + 1, 1 - p, m - TURN)

            walk_tiles(pe, TILES, tile)
            for m in range(FC - LAG, FC):
                second(TILES - 1, m)

        @block.scalar
        def _(act):
            for i, (st, dst, _) in enumerate(pieces):
                act.wait_ge(w_loaded, 16 * (5 + i))
                act.activation(dst[:, HIGH], st, ACT.Copy).then_inc(w_high, 1)

            def high_hT(t, p, c):
                at_least(act, hT_psum, t * DC + c + 1)
                act.activation(hT[:, p, HIGH, c, :], x_bank[:, (p + c) % 2, :], ACT.Copy).then_inc(hT_high, 1)

            for c in range(DC):
                high_hT(0, 0, c)

            def tile(t, pair, p):
                for m in range(FC):
                    n = t * FC + m
                    at_least(act, f_ready, n + 1)
                    at_least(act, g_low, n - 1)
                    act.activation(act_out[:, m % 2, :], f_bank[:, m % 2, :], ACT.Silu,
                                   bias=b1_c[:, m:m + 1]).then_inc(silu_done, 1)
                    at_least(act, silu_done, n + 1)
                    act.activation(gT[:, m % RING, HIGH, :], act_out[:, m % 2, :], ACT.Copy).then_inc(g_high, 1)
                    if TURN <= m < TURN + DC and not is_last(t):
                        high_hT(t + 1, 1 - p, m - TURN)

            walk_tiles(act, TILES, tile)

        @block.vector
        def _(dve):
            dve.memset(minus_half[:, :], -0.5).then_inc(const_made, 1)
            for i, (st, dst, _) in enumerate(pieces):
                dve.wait_ge(w_high, i + 1)
                dve.tensor_tensor(dst[:, LOW], st, dst[:, HIGH].bitcast(F32), ALU.subtract).then_inc(w_low, 1)

            def low_hT(t, p, c):
                at_least(dve, hT_high, t * DC + c + 1)
                dve.tensor_tensor(hT[:, p, LOW, c, :], x_bank[:, (p + c) % 2, :],
                                  hT[:, p, HIGH, c, :].bitcast(F32), ALU.subtract).then_inc(hT_low, 1)

            for c in range(DC):
                low_hT(0, 0, c)

            def moments(src, which, g, ready, count, stats_done, done):
                at_least(dve, ready, count)
                dve.bn_stats(stats[:, which, g, :], src[:, g, :]).then_inc(stats_done, 1)
                at_least_apart(dve, stats_done, count, dve_passed)
                dve.bn_aggr(mean_var[:, which, g, :], stats[:, which, g, :]).then_inc(done, 1)

            def add_residual(t, p, g):
                at_least(dve, y_psum, t * G + g + 1)
                at_least(dve, sums_ready, 2 * t + 1)
                dve.tensor_tensor(y[:, g, :], y_bank[:, g, 0:D], hb[:, p, g, :], ALU.add).then_inc(y_ready, 1)

            def second_sum(t, p, g):
                at_least(dve, rms_ready, t + 1)
                at_least(dve, sums_ready, 2 * t + 2)
                at_least(dve, fin_ready, t * G)
                dve.scalar_tensor_tensor(out=z[:, g, :], in0=y[:, g, :], scalar=ms[:, 2, g:g + 1], in1=alpha_b[:, :],
                                         op0=ALU.mult, op1=ALU.mult).then_inc(y_scaled, 1)
                at_least(dve, y_scaled, t * G + g + 1)
                dve.tensor_tensor(z[:, g, :], z[:, g, :], xg[:, p, g, :], ALU.add).then_inc(z_ready, 1)

            def after(t, p, step):
                if step == 1:
                    for g in range(G):
                        add_residual(t, p, g)
                elif step == 2:
                    for g in range(G):
                        moments(y, 0, g, y_ready, t * G + g + 1, y_stats, y_moments)
                elif 4 <= step < 4 + G:
                    second_sum(t, p, step - 4)
                    moments(z, 1, step - 4, z_ready, t * G + step - 4 + 1, z_stats, z_moments)

            def tile(t, pair, p):
                for m in range(FC):
                    n = t * FC + m
                    at_least(dve, g_high, n + 1)
                    dve.tensor_tensor(gT[:, m % RING, LOW, :], act_out[:, m % 2, :],
                                      gT[:, m % RING, HIGH, :].bitcast(F32), ALU.subtract).then_inc(g_low, 1)
                    if TURN <= m < TURN + DC and not is_last(t):
                        low_hT(t + 1, 1 - p, m - TURN)
                    if not (isinstance(t, int) and t == 0):
                        after(t - 1, 1 - p, m)

            walk_tiles(dve, TILES, tile)
            for step in range(FC):
                after(TILES - 1, 1, step)

        @block.gpsimd
        def _(pool):
            pool.memset(ident[:, :], 0.0).then_inc(pool_step, 1)
            pool.wait_ge(pool_step, 1)
            pool.affine_select(out=ident[:, :], in_=ident[:, :], compare_op=ALU.not_equal, fill=1.0,
                               base=0, pattern=[[-1, P]], channel_multiplier=1).then_inc(const_made, 1)
            pool.wait_ge(w_low, 4)
            pool.wait_ge(w_loaded, 16 * 8)
            pool.wait_ge(const_made, 2)
            STEPS = 5

            def sums(t, p):
                at_least(pool, h_loaded, 16 * (t + 1))
                at_least(pool, y_ready, G * (t - 1))
                pool.tensor_tensor(hb[:, p, :, :], h_nat[:, :, :], b2_b[:, :].unsqueeze(1).to_broadcast([P, G, D]),
                                   ALU.add).then_inc(sums_ready, 1)
                at_least(pool, x_loaded, 16 * (t + 1))
                at_least(pool, z_ready, G * (t - 1))
                pool.tensor_tensor(xg[:, p, :, :], x_nat[:, :, :], gamma_b[:, :].unsqueeze(1).to_broadcast([P, G, D]),
                                   ALU.add).then_inc(sums_ready, 1)

            def norms(t):
                done = 1 + t * STEPS
                at_least(pool, y_moments, (t + 1) * G)
                mean, var = mean_var[:, 0, :, 0], mean_var[:, 0, :, 1]
                pool.tensor_tensor(ms[:, 0, :], mean, mean, ALU.mult).then_inc(pool_step, 1)
                at_least(pool, pool_step, done + 1)
                pool.tensor_tensor(ms[:, 1, :], ms[:, 0, :], var, ALU.add).then_inc(pool_step, 1)
                at_least_apart(pool, pool_step, done + 2, pool_passed)
                pool.tensor_scalar(ms[:, 0, :], ms[:, 1, :], RMS_EPS, None, ALU.add).then_inc(pool_step, 1)
                at_least(pool, pool_step, done + 3)
                at_least(pool, y_scaled, t * G)
                pool.tensor_tensor(ms[:, 2, :], ms[:, 0, :], minus_half[:, :], ALU.pow).then_inc(rms_ready, 1)
                at_least_apart(pool, z_moments, (t + 1) * G, pool_passed)
                mean, var = mean_var[:, 1, :, 0], mean_var[:, 1, :, 1]
                pool.tensor_scalar(ms[:, 3, :], var, LN_EPS, None, ALU.add).then_inc(pool_step, 1)
                at_least(pool, pool_step, done + 4)
                pool.tensor_tensor(ms[:, 4, :], ms[:, 3, :], minus_half[:, :], ALU.pow).then_inc(pool_step, 1)
                at_least_apart(pool, pool_step, done + 5, pool_passed)

            def finish(t, g):
                mean = mean_var[:, 1, g, 0:1]
                at_least_apart(pool, stored, 16 * t, pool_passed)
                pool.tensor_scalar(ms[:, 5, g:g + 1], mean, ms[:, 4, g:g + 1], -1.0, ALU.mult, ALU.mult).then_inc(shift_ready, 1)
                at_least_apart(pool, shift_ready, t * G + g + 1, pool_passed)
                pool.tensor_scalar(o_nat[:, g, :], z[:, g, :], ms[:, 4, g:g + 1], ms[:, 5, g:g + 1],
                                   ALU.mult, ALU.add).then_inc(fin_ready, 1)

            sums(0, 0)

            def tile(t, pair, p):
                if not (isinstance(t, int) and t == 0):
                    norms(t - 1)
                    for g in range(G):
                        finish(t - 1, g)
                if not is_last(t):
                    sums(t + 1, 1 - p)

            walk_tiles(pool, TILES, tile)
            norms(TILES - 1)
            for g in range(G):
                finish(TILES - 1, g)


def build(nc, x, adj, q0, k0, v0, bv0, o0, bo0, q1, bq1, k1, bk1, v1, bv1, o1, bo1,
          w1, b1, w2, b2, alpha1, gamma1, alpha2, gamma2, out):
    x1 = nc.dram_tensor("x1", x.shape, F32, kind="Internal").ap()
    h1 = nc.dram_tensor("h1", x.shape, F32, kind="Internal").ap()
    attention_pass(nc, "a0", x, adj, q0, k0, v0, o0, None, None, bv0, bo0, None, None, x1, 12, True)
    attention_pass(nc, "a1", x1, adj, q1, k1, v1, o1, bq1, bk1, bv1, bo1, alpha1, gamma1, h1, 8, False)
    feed_forward_pass(nc, x1, h1, w1, b1, w2, b2, alpha2, gamma2, out)


_INS = ['x', 'adj', 'L0_gnn_Wq', 'L0_gnn_Wk', 'L0_gnn_Wv', 'L0_gnn_bv', 'L0_gnn_Wo', 'L0_gnn_bo',
        'L1_gnn_wq', 'L1_gnn_bq', 'L1_gnn_wk', 'L1_gnn_bk', 'L1_gnn_wv', 'L1_gnn_bv', 'L1_gnn_wo', 'L1_gnn_bo',
        'L1_gnn_w1', 'L1_gnn_b1', 'L1_gnn_w2', 'L1_gnn_b2', 'L1_gnn_alpha1', 'L1_gnn_gamma1',
        'L1_gnn_alpha2', 'L1_gnn_gamma2']
_TURNED = ['L0_gnn_Wq', 'L0_gnn_Wk', 'L0_gnn_Wv', 'L0_gnn_Wo']


def kernel(**inputs):
    import numpy as _np
    import concourse.bacc as _bacc
    from concourse import mybir as _mybir
    from concourse.bass_utils import run_bass_kernel_spmd as _run

    nc = _bacc.Bacc("TRN2", target_bir_lowering=False, num_devices=1)
    arrays, args = {}, []
    for name in _INS:
        a = _np.asarray(inputs[name])
        a = _np.ascontiguousarray(a.T if name in _TURNED else a)
        arrays[f"in_{name}_dram"] = a
        args.append(nc.dram_tensor(f"in_{name}_dram", a.shape, _mybir.dt.from_np(a.dtype), kind="ExternalInput").ap())
    args.append(nc.dram_tensor("out_dram", (64, 128, 384), _mybir.dt.float32, kind="ExternalOutput").ap())
    build(nc, *args)
    r = _run(nc, [arrays], core_ids=[0])
    return r.results[0]["out_dram"]
```

```python
from contextlib import ExitStack

import concourse.bass as bass
from concourse import mybir

F32 = mybir.dt.float32
F32R = mybir.dt.float32r
ALU = mybir.AluOpType
ACT = mybir.ActivationFunctionType
AX = mybir.AxisListType

P = 128
D = 384
DC = D // P
G = 4
TOK = G * P
HIGH, LOW = 0, 1
PARTS = [(HIGH, HIGH), (HIGH, LOW), (LOW, HIGH)]
LOWEST = -3.4028234663852886e38
LN_EPS = 1e-5
RMS_EPS = 1e-6


def at_least(eng, sem, value):
    if isinstance(value, int) and value <= 0:
        return
    eng.wait_ge(sem, value)


def at_least_apart(eng, sem, value, passed):
    if isinstance(value, int):
        at_least(eng, sem, value)
    else:
        eng.wait_ge(sem, value)
        eng.sem_inc(passed, 1)


def walk_tiles(eng, tiles, body):
    for p in range(2):
        body(p, 0, p)
    with eng.Fori(1, tiles // 2 - 1) as pair:
        for p in range(2):
            body(pair * 2 + p, pair, p)
    for p in range(2):
        body(tiles - 2 + p, tiles // 2 - 1, p)


def attention_pass(nc, tag, x_in, xT_in, adj_in, wq_in, wk_in, wv_in, wo_in, bq_in, bk_in, bv_in, bo_in,
                   alpha_in, gamma_in, out, heads, masked,
                   x_nat, x_loaded, x_ahead, ahead, stored, stored_before):
    B = x_in.shape[0]
    TILES = B // G
    DH = D // heads
    SCALE = float(D if masked else DH) ** -0.5
    HB = 4
    NB = heads // HB
    DHP = 32 if DH == 32 else 64
    OC = heads * DHP // P
    HPC = P // DHP
    blocks = []
    for c in range(DC):
        for h in range(heads):
            r0, r1 = max(h * DH, c * P), min((h + 1) * DH, (c + 1) * P)
            if r0 < r1:
                blocks.append((c, h, r0 - c * P, r1 - r0))
    NBLK = len(blocks)
    runs = []
    for i, (c, h, _, _) in enumerate(blocks):
        if runs and runs[-1][0] == c and h // HB == runs[-1][3] // HB:
            runs[-1][2] += 1
        else:
            runs.append([c, i, 1, h])
    biased = bq_in is not None
    rms = alpha_in is not None

    given = xT_in is not None
    XS = 0 if given else DC
    USE = {"X": 0, "K": XS, "Q": XS + DC, "V": XS + 2 * DC}
    USES = XS + 2 * DC + G
    HIGHS = XS + 2 * DC
    XP = 2 if given else 1

    with ExitStack() as ctx:
        def sb(name, shape, dt=F32):
            return ctx.enter_context(nc.sbuf_tensor(f"{tag}_{name}", shape, dt))

        def sem(name):
            return ctx.enter_context(nc.semaphore(f"{tag}_{name}"))

        ident = sb("ident", [P, P])
        w_qkv = [sb(f"w_{n}", [P, 2, DC, D], F32R) for n in "qkv"]
        w_o = sb("w_o", [P, 2, OC, D], F32R)
        bv_b = sb("bv_b", [P, D])
        bo_b = sb("bo_b", [P, D])
        if biased:
            bq_c = sb("bq_c", [P, DC])
            bqs_c = sb("bqs_c", [P, DC])
            bk_c = sb("bk_c", [P, DC])
        if rms:
            alpha_b = sb("alpha_b", [P, D])
            gamma_b = sb("gamma_b", [P, D])
        xb = sb("xb", [P, 2, D])
        adj = sb("adj", [P, 2, G, P])
        xT = sb("xT", [P, XP, 2, DC, TOK], F32R)
        if given:
            xT_raw = sb("xT_raw", [P, 2, TOK])
        qT = sb("qT", [P, 2, 2, DC, TOK], F32R)
        kT = sb("kT", [P, 2, 2, DC, TOK], F32R)
        k_blk = sb("k_blk", [P, 2, 2, NBLK, P], F32R)
        v = sb("v", [P, 2, G, heads, DHP])
        scores = sb("scores", [P, heads, P])
        probs = sb("probs", [P, 2, heads, P])
        pT = sb("pT", [P, max(heads, OC * 3), P])
        oT = sb("oT", [P, 2, OC, P], F32R)
        y = sb("y", [P, 2, D])
        o_nat = sb("o_nat", [P, 2, D])
        row_max = sb("row_max", [P, 2, heads])
        neg_max = sb("neg_max", [P, 2, heads])
        row_abs = sb("row_abs", [P, 2, heads])
        row_sum = sb("row_sum", [P, 2, heads])
        inv_sum = sb("inv_sum", [P, 2, heads])
        weight = sb("weight", [P, 2, heads])
        stats = sb("stats", [P, 6])
        mean_var = sb("mean_var", [P, 2, 2])
        scalars = sb("scalars", [P, 4])
        minus_half = sb("minus_half", [P, 1])

        bank = ctx.enter_context(nc.psum_tensor(f"{tag}_bank", [P, 8, 512], F32))
        s_bank = bank[:, 0:NB, :]
        t_bank = bank[:, 3:5, :]
        j_bank = bank[:, 5:7, :]
        o_bank = bank[:, 7, :]

        w_loaded = [sem(f"w_loaded{i}") for i in range(4)]
        vectors_loaded = sem("vectors_loaded")
        bias_scaled = sem("bias_scaled")
        blk_zeroed = sem("blk_zeroed")
        zeroed = sem("zeroed")
        const_made = sem("const_made")
        w_high = sem("w_high")
        w_low = sem("w_low")
        xT_staged = [sem(f"xT_staged{i}") for i in range(2)]
        xT_loaded = [sem(f"xT_loaded{i}") for i in range(2)]
        xT_high = sem("xT_high")
        xT_low = sem("xT_low")
        adj_loaded = [sem(f"adj_loaded{i}") for i in range(2)]
        k_blk_loaded = [sem(f"k_blk_loaded{i}") for i in range(2)]
        j_ready = sem("j_ready")
        s_ready = sem("s_ready")
        t_ready = sem("t_ready")
        pv_ready = sem("pv_ready")
        op_ready = sem("op_ready")
        high_done = sem("high_done")
        exp_done = sem("exp_done")
        pT_ready = sem("pT_ready")
        o_high_done = sem("o_high_done")
        j_done = sem("j_done")
        s_read = sem("s_read")
        neg_max_ready = sem("neg_max_ready")
        abs_done = sem("abs_done")
        inv_ready = sem("inv_ready")
        weight_ready = sem("weight_ready")
        o_low_done = sem("o_low_done")
        y_ready = sem("y_ready")
        stats_ready = sem("stats_ready")
        mean_var_ready = sem("mean_var_ready")
        xb_ready = sem("xb_ready")
        probs_ready = sem("probs_ready")
        pool_step = sem("pool_step")
        fin_ready = sem("fin_ready")
        dve_passed, pool_passed, sp_passed = sem("dve_passed"), sem("pool_passed"), sem("sp_passed")

        x_v = x_in.rearrange("(t g) p d -> t p g d", g=G)
        adj_v = adj_in.rearrange("(t g) p k -> t p g k", g=G)
        out_v = out.rearrange("(t g) p d -> t g p d", g=G)

        if given:
            xT_v = xT_in.rearrange("(c p) (t n) -> t p c n", p=P, n=TOK)

        second = scores[:, :, :].rearrange("p h k -> p (h k)") if given else x_nat[:, 1, :, :].rearrange("p g d -> p (g d)")
        stage = [probs[:, :, :, :].rearrange("p a h k -> p (a h k)")[:, 0:DC * D].rearrange("p (c d) -> p c d", c=DC),
                 second[:, 0:DC * D].rearrange("p (c d) -> p c d", c=DC),
                 v[:, :, :, :, :].rearrange("p a g h d -> p (a g h d)")[:, 0:DC * D].rearrange("p (c d) -> p c d", c=DC),
                 pT[:, :, :].rearrange("p h k -> p (h k)")[:, 0:OC * D].rearrange("p (c d) -> p c d", c=OC)]

        FIRST = [("X", c) for c in range(XS)] + [(k, c) for k in "KQ" for c in range(DC)] + [("V", g) for g in range(G)]
        if given:
            EARLY = [[], [], [], []]
            BEFORE = [[("K", 0)], [("K", 2)], [("Q", 1), ("Q", 2)], [("V", 1)]]
            AFTER = [[("K", 1)], [("Q", 0)], [("V", 0)], [("V", 2), ("V", 3)]]
            EXPS = [{"start": 10, "pT": 12}] * G
        else:
            EARLY = [[("X", 0), ("X", 1)], [], [], []]
            BEFORE = [[("X", 2)], [("K", 2), ("Q", 0)], [("Q", 2), ("V", 0)], [("V", 2)]]
            AFTER = [[("K", 0), ("K", 1)], [("Q", 1)], [("V", 1)], [("V", 3)]]
            EXPS = [{("X", 1): 4, "pT": 8, ("K", 0): 12}, {"start": 5, ("K", 2): 9, "pT": 12},
                    {"start": 5, ("Q", 2): 8, "pT": 12}, {"start": 4, "pT": 12}]
        is_last = lambda t: isinstance(t, int) and t == TILES - 1

        block = ctx.enter_context(nc.Block())

        weights = [(stage[0], wk_in, w_qkv[1], 1.0), (stage[1], wq_in, w_qkv[0], SCALE),
                   (stage[2], wv_in, w_qkv[2], 1.0), (stage[3], wo_in, w_o, 1.0)]
        W_READY = {"K": 1, "Q": 2, "V": 3, "O": 4}
        vectors = [(bv_b, bv_in), (bo_b, bo_in)] + ([(alpha_b, alpha_in), (gamma_b, gamma_in)] if rms else [])
        columns = [(bq_c, bq_in), (bk_c, bk_in)] if biased else []
        n_vectors = len(vectors) + len(columns)
        n_wo = 1 if DHP == DH else heads

        @block.sync
        def _(sp):
            def load_w(i):
                st, w, _, _ = weights[i]
                sp.dma_start(st, w.rearrange("(c p) n -> p c n", p=P)).then_inc(w_loaded[i], 16)

            def load_x(t, p):
                sp.dma_start(x_nat[:, p, :, :], x_v[bass.ds(t, 1)].rearrange("a p g d -> p (a g) d")).then_inc(x_loaded[p], 16)

            def stage_xT(t):
                sp.dma_start(x_nat[:, t, :, :].rearrange("p g d -> p (g d)"),
                             xT_v[t]).then_inc(xT_staged[t], 16)

            def load_xT(t, p, c):
                at_least_apart(sp, xT_low, (t + 2) * DC + c - 1, sp_passed)
                if c == 0:
                    at_least_apart(sp, j_ready, (t + 1) * USES, sp_passed)
                sp.dma_start(xT_raw[:, (p * DC + c) % 2, :], xT_v[bass.ds(t + 2, 1), :, c].rearrange("a p n -> p (a n)")).then_inc(xT_loaded[(p * DC + c) % 2], 16)

            def load_adj(t, p):
                sp.dma_start(adj[:, p, :, :], adj_v[bass.ds(t, 1)].rearrange("a p g d -> p (a g) d")).then_inc(adj_loaded[p], 16)

            def load_k_blk(t, p, g):
                n = t * G + g
                at_least_apart(sp, high_done, t * HIGHS + USE["Q"], sp_passed)
                at_least_apart(sp, j_done, t * USES + USE["Q"], sp_passed)
                at_least_apart(sp, s_ready, (n - 1) * NB, sp_passed)
                if DH == 32:
                    for j in range(HB):
                        r = j * DH
                        sp.dma_start(
                            k_blk[r:r + DH, g % 2, :, :, :].rearrange("p s (c j) k -> p (s c) j k", j=HB)[:, :, j, :].bitcast(F32),
                            kT[r:r + DH, p, :, :, g * P:(g + 1) * P].rearrange("p s c k -> p (s c) k").bitcast(F32),
                        ).then_inc(k_blk_loaded[g % 2], 16)
                else:
                    for i, (c, _, r, rows) in enumerate(blocks):
                        sp.dma_start(k_blk[r:r + rows, g % 2, :, i, :].bitcast(F32),
                                     kT[r:r + rows, p, :, c, g * P:(g + 1) * P].bitcast(F32)).then_inc(k_blk_loaded[g % 2], 16)

            def store(t, g):
                n = t * G + g
                at_least_apart(sp, fin_ready, n + 1, sp_passed)
                sp.dma_start(out_v[bass.ds(t, 1), g].rearrange("a p d -> p (a d)"), o_nat[:, g % 2, :]).then_inc(stored[g % 2], 16)

            load_w(0)
            if given:
                stage_xT(0)
            elif not x_ahead:
                load_x(0, 0)
            load_w(1)
            for dst, src in columns:
                with nc.allow_non_contiguous_dma(reason="bias columns, 384 elements once"):
                    sp.dma_start(dst[:, :], src.rearrange("(c p) -> p c", p=P)).then_inc(vectors_loaded, 16)
            for dst, src in vectors:
                sp.dma_start(dst[:, :], src.rearrange("(a d) -> a d", a=1).to_broadcast([P, D])).then_inc(vectors_loaded, 16)
            load_w(2)
            load_adj(0, 0)
            if given:
                stage_xT(1)
            if DHP == DH:
                load_w(3)
            else:
                sp.wait_ge(zeroed, 2)
                for h in range(heads):
                    r = (h % HPC) * DHP
                    sp.dma_start(stage[3][r:r + DH, h // HPC, :], wo_in[h * DH:(h + 1) * DH, :]).then_inc(w_loaded[3], 16)
            sp.wait_ge(blk_zeroed, 1)
            load_k_blk(0, 0, 0)
            sp.wait_ge(blk_zeroed, 2)
            load_k_blk(0, 0, 1)
            if given:
                for i in range(2):
                    sp.wait_ge(xT_low, (i + 1) * DC)
                    load_x(i, i)
            else:
                sp.wait_ge(w_low, 2)
                for done in stored_before:
                    sp.wait_ge(done, 16 * B // 2)
                load_x(1, 1)
            load_adj(1, 1)

            def tile(t, pair, p):
                for g in range(G):
                    if not (is_last(t) and g >= 2):
                        load_k_blk(t + (g + 2) // G, (p + (g + 2) // G) % 2, (g + 2) % G)
                    if is_last(t) and g == 2:
                        sp.wait_ge(xb_ready, (TILES - 1) * G)
                        for i in range(2):
                            sp.wait_ge(stored[i], 16 * (TILES - 1) * G // 2)
                        for dst, src, loaded in ahead:
                            sp.dma_start(dst, src).then_inc(loaded, 16)
                    more = not (isinstance(t, int) and t >= TILES - 2)
                    if g < DC and more and given:
                        load_xT(t, p, g)
                    if g == 3 and more:
                        at_least_apart(sp, xb_ready, (t + 1) * G, sp_passed)
                        load_x(t + 2, p)
                    if g == 3 and more:
                        at_least_apart(sp, s_read, (t * G + G) * NB, sp_passed)
                        load_adj(t + 2, p)
                    if g >= 2:
                        store(t, g - 2)
                    elif not (isinstance(t, int) and t == 0):
                        store(t - 1, g + 2)

            walk_tiles(sp, TILES, tile)
            store(TILES - 1, 2)
            store(TILES - 1, 3)

        @block.tensor
        def _(pe):
            def free_j(u):
                at_least(pe, j_done, u - 1)

            def have_xT(t):
                if given:
                    at_least(pe, xT_low, (t + 1) * DC)
                else:
                    at_least(pe, j_done, t * USES + XS)

            def project(t, pair, p, kind, i):
                u = t * USES + USE[kind] + i
                dst = j_bank[:, (p * USES + USE[kind] + i) % 2, :]
                if kind == "X":
                    if i == 0:
                        at_least(pe, x_loaded[p], 16 * (pair + 1))
                    free_j(u)
                    for g in range(G):
                        mm = pe.transpose(dst[:, g * P:(g + 1) * P], x_nat[:, p, g, i * P:(i + 1) * P], ident[:, :])
                elif kind in "QK":
                    have_xT(t)
                    free_j(u)
                    w = w_qkv["QK".index(kind)]
                    todo = [(c, a, b) for c in range(DC) for a, b in PARTS]
                    for k, (c, a, b) in enumerate(todo):
                        mm = pe.matmul(dst, w[:, a, c, i * P:(i + 1) * P], xT[:, p % XP, b, c, :],
                                       start=k == 0, stop=k == len(todo) - 1)
                else:
                    have_xT(t)
                    free_j(u)
                    todo = [(c, a, b) for c in range(DC) for a, b in PARTS]
                    for k, (c, a, b) in enumerate(todo):
                        mm = pe.matmul(dst[:, 0:D], xT[:, p % XP, a, c, i * P:(i + 1) * P], w_qkv[2][:, b, c, :],
                                       start=k == 0, stop=k == len(todo) - 1)
                mm.then_inc(j_ready, 1)

            def score(t, p, g):
                n = t * G + g
                at_least(pe, k_blk_loaded[g % 2], 16 * (HB if DH == 32 else NBLK) * (t * 2 + g // 2 + 1))
                at_least(pe, j_done, t * USES + USE["V"])
                for b in range(NB):
                    mine = [r for r in runs if r[3] // HB == b]
                    at_least(pe, s_read, (n - 1) * NB + b + 1)
                    for k, (c, i, m, h) in enumerate(mine):
                        for a, part in enumerate(PARTS):
                            col = (h % HB) * P
                            mm = pe.matmul(s_bank[:, b, col:col + m * P], qT[:, p, part[0], c, g * P:(g + 1) * P],
                                           k_blk[:, g % 2, part[1], i:i + m, :],
                                           start=k == 0 and a == 0, stop=k == len(mine) - 1 and a == 2,
                                           skip_group_check=len(mine) > 1)
                    mm.then_inc(s_ready, 1)

            def turn(t, g, banks):
                n = t * G + g
                for q in banks:
                    at_least(pe, probs_ready, n * NB + q + 1)
                    at_least(pe, pT_ready, n * NB + q - 1)
                    for j in range(HB):
                        mm = pe.transpose(t_bank[:, (NB * g + q) % 2, j * P:(j + 1) * P],
                                          probs[:, g % 2, q * HB + j, :], ident[:, :])
                    mm.then_inc(t_ready, 1)

            def attend(t, p, g):
                n = t * G + g
                at_least(pe, j_done, t * USES + USE["V"] + g + 1)
                at_least(pe, y_ready, n)
                for h in range(heads):
                    if h % HB == 0:
                        at_least(pe, pT_ready, n * NB + h // HB + 1)
                    r = (h % HPC) * DHP
                    c = h // HPC
                    mm = pe.matmul(o_bank[r:r + DHP, c * P:(c + 1) * P], v[:, p, g, h, :], pT[:, h, :],
                                   start=True, stop=True)
                mm.then_inc(pv_ready, 1)

            def output(t, g):
                n = t * G + g
                if isinstance(t, int) and t == 0 and g == 0:
                    pe.wait_ge(w_low, W_READY["O"])
                at_least(pe, o_low_done, n + 1)
                todo = [(c, a, b) for c in range(OC) for a, b in PARTS]
                for k, (c, a, b) in enumerate(todo):
                    mm = pe.matmul(o_bank[:, 0:D], oT[:, a, c, :], w_o[:, b, c, :],
                                   start=k == 0, stop=k == len(todo) - 1)
                mm.then_inc(op_ready, 1)

            pe.wait_ge(const_made, 2)
            for kind, i in FIRST:
                if kind != "X" and i == 0:
                    pe.wait_ge(w_low, W_READY[kind])
                project(0, 0, 0, kind, i)
                if (kind, i) == ("V", 0):
                    score(0, 0, 0)

            def tile(t, pair, p):
                for g in range(G):
                    last = is_last(t)
                    if g < G - 1:
                        score(t, p, g + 1)
                    elif not last:
                        score(t + 1, 1 - p, 0)
                    if not last:
                        for kind, i in EARLY[g]:
                            project(t + 1, pair + p, 1 - p, kind, i)
                    if g > 0:
                        output(t, g - 1)
                    elif not (isinstance(t, int) and t == 0):
                        output(t - 1, G - 1)
                    if not last:
                        for kind, i in BEFORE[g]:
                            project(t + 1, pair + p, 1 - p, kind, i)
                    turn(t, g, range(0, 2))
                    if not last:
                        for kind, i in AFTER[g]:
                            project(t + 1, pair + p, 1 - p, kind, i)
                    turn(t, g, range(2, NB))
                    attend(t, p, g)

            walk_tiles(pe, TILES, tile)
            output(TILES - 1, G - 1)

        @block.scalar
        def _(act):
            def high_w(i):
                st, _, dst, scale = weights[i]
                act.wait_ge(w_loaded[i], 16 * (n_wo if i == 3 else 1))
                act.activation(dst[:, HIGH, :, :], st, ACT.Copy, scale=scale).then_inc(w_high, 1)

            def high(t, p, kind, i):
                at_least(act, j_ready, t * USES + USE[kind] + i + 1)
                src = j_bank[:, (p * USES + USE[kind] + i) % 2, :]
                if kind == "X":
                    op = act.activation(xT[:, 0, HIGH, i, :], src, ACT.Copy)
                else:
                    dst = (qT if kind == "Q" else kT)[:, p, HIGH, i, :]
                    if biased:
                        op = act.activation(dst, src, ACT.Identity, bias=(bqs_c if kind == "Q" else bk_c)[:, i:i + 1])
                    else:
                        op = act.activation(dst, src, ACT.Copy)
                op.then_inc(high_done, 1)

            def exp(t, g, h):
                n = t * G + g
                if h % HB == 0:
                    at_least(act, neg_max_ready, n * NB + h // HB + 1)
                if h == 0:
                    at_least(act, t_ready, (n - 1) * NB)
                op = act.activation(probs[:, g % 2, h, :], scores[:, h, :], ACT.Exp,
                                    bias=neg_max[:, g % 2, h:h + 1], accum_out=row_sum[:, g % 2, h:h + 1])
                if h % HB == HB - 1:
                    op.then_inc(exp_done, 1)

            def copy_pT(t, g, q):
                n = t * G + g
                at_least(act, t_ready, n * NB + q + 1)
                act.activation(pT[:, q * HB:(q + 1) * HB, :].rearrange("p h k -> p (h k)"),
                               t_bank[:, (NB * g + q) % 2, :], ACT.Copy).then_inc(pT_ready, 1)

            def high_o(t, g):
                at_least(act, pv_ready, t * G + g + 1)
                act.activation(oT[:, HIGH, :, :].rearrange("p c k -> p (c k)"), o_bank[:, 0:OC * P],
                               ACT.Copy).then_inc(o_high_done, 1)

            def high_xT(pair, p, c):
                k = p * DC + c
                at_least(act, xT_loaded[k % 2], 16 * (pair * DC + k // 2 + 1))
                act.activation(xT[:, p, HIGH, c, :], xT_raw[:, k % 2, :], ACT.Copy).then_inc(xT_high, 1)

            def high_staged(i, c):
                act.wait_ge(xT_staged[i], 16)
                act.activation(xT[:, i, HIGH, c, :], x_nat[:, i, :, :].rearrange("p g d -> p (g d)")[:, c * TOK:(c + 1) * TOK],
                               ACT.Copy).then_inc(xT_high, 1)

            if given:
                high_w(0)
            for c in range(DC):
                if given:
                    high_staged(0, c)
                else:
                    high(0, 0, "X", c)
            if not given:
                high_w(0)
            high_w(1)
            if biased:
                act.wait_ge(vectors_loaded, 16 * n_vectors)
                act.activation(bqs_c[:, :], bq_c[:, :], ACT.Copy, scale=SCALE).then_inc(bias_scaled, 1)
                act.wait_ge(bias_scaled, 1)
            for kind, i in FIRST:
                if kind in "KQ":
                    high(0, 0, kind, i)
                if (kind, i) == ("K", 0):
                    high_w(2)
            high_w(3)
            for c in range(DC):
                if given:
                    high_staged(1, c)
            for h in range(heads):
                exp(0, 0, h)

            def tile(t, pair, p):
                for g in range(G):
                    last = is_last(t)
                    nt, ng = (t, g + 1) if g < G - 1 else (t + 1, 0)
                    done = 0

                    def exps(mark):
                        nonlocal done
                        if not (last and g == G - 1):
                            upto = heads * EXPS[g].get(mark, 0) // 12
                            for h in range(done, upto):
                                exp(nt, ng, h)
                            done = max(done, upto)

                    def highs(uses):
                        for kind, i in uses:
                            if kind != "V" and not last:
                                high(t + 1, 1 - p, kind, i)
                            exps((kind, i))

                    if given and g > 0 and not (isinstance(t, int) and t >= TILES - 2):
                        high_xT(pair, p, g - 1)
                    exps("start")
                    highs(EARLY[g] + BEFORE[g])
                    for q in range(0, 2):
                        copy_pT(t, g, q)
                    exps("pT")
                    for q in range(2, NB):
                        copy_pT(t, g, q)
                    exps("pT end")
                    highs(AFTER[g])
                    high_o(t, g)

            walk_tiles(act, TILES, tile)

        @block.vector
        def _(dve):
            dve.memset(minus_half[:, :], -0.5).then_inc(zeroed, 1)
            if DHP != DH:
                dve.memset(stage[3], 0.0).then_inc(zeroed, 1)

            def low_w(i):
                st, _, dst, scale = weights[i]
                dve.wait_ge(w_high, i + 1)
                dve.scalar_tensor_tensor(out=dst[:, LOW, :, :], in0=st, scalar=scale,
                                         in1=dst[:, HIGH, :, :].bitcast(F32), op0=ALU.mult,
                                         op1=ALU.subtract).then_inc(w_low, 1)

            def evacuate(t, p, kind, i):
                u = t * USES + USE[kind] + i
                src = j_bank[:, (p * USES + USE[kind] + i) % 2, :]
                if kind == "V":
                    at_least(dve, j_ready, u + 1)
                    op = dve.tensor_tensor(v[:, p, i, :, 0:DH], src[:, 0:D].rearrange("p (h d) -> p h d", h=heads),
                                           bv_b[:, :].rearrange("p (h d) -> p h d", h=heads), ALU.add)
                else:
                    at_least(dve, high_done, t * HIGHS + USE[kind] + i + 1)
                    if kind == "X":
                        dst, hi = xT[:, 0, LOW, i, :], xT[:, 0, HIGH, i, :]
                    else:
                        k = qT if kind == "Q" else kT
                        dst, hi = k[:, p, LOW, i, :], k[:, p, HIGH, i, :]
                    if biased and kind != "X":
                        op = dve.scalar_tensor_tensor(out=dst, in0=src, scalar=(bqs_c if kind == "Q" else bk_c)[:, i:i + 1],
                                                      in1=hi.bitcast(F32), op0=ALU.add, op1=ALU.subtract)
                    else:
                        op = dve.tensor_tensor(dst, src, hi.bitcast(F32), ALU.subtract)
                op.then_inc(j_done, 1)

            def add_adjacency(t, pair, p, g):
                n = t * G + g
                if g == 0:
                    at_least(dve, adj_loaded[p], 16 * (pair + 1))
                at_least(dve, exp_done, n * NB)
                if masked:
                    at_least(dve, abs_done, n)
                for h in range(heads):
                    if h % HB == 0:
                        at_least_apart(dve, s_ready, n * NB + h // HB + 1, dve_passed)
                    op = dve.tensor_tensor_reduce(out=scores[:, h, :], in0=s_bank[:, h // HB, (h % HB) * P:(h % HB + 1) * P],
                                                  in1=adj[:, p, g, :], scale=1.0, scalar=LOWEST, op0=ALU.add,
                                                  op1=ALU.max, accum_out=row_max[:, g % 2, h:h + 1])
                    if h % HB == HB - 1:
                        op.then_inc(s_read, 1)
                    if h % HB == HB - 1:
                        q = h // HB
                        at_least(dve, s_read, n * NB + q + 1)
                        dve.tensor_scalar(neg_max[:, g % 2, q * HB:(q + 1) * HB], row_max[:, g % 2, q * HB:(q + 1) * HB],
                                          -1.0, None, ALU.mult).then_inc(neg_max_ready, 1)

            def largest(t, g):
                dve.tensor_reduce(row_abs[:, g % 2, :], scores[:, :, :], AX.X, ALU.max,
                                  apply_absolute_value=True).then_inc(abs_done, 1)

            def weigh(t, g):
                n = t * G + g
                at_least(dve, exp_done, (n + 1) * NB)
                dst = inv_sum if masked else weight
                dve.reciprocal(dst[:, g % 2, :], row_sum[:, g % 2, :]).then_inc(inv_ready if masked else weight_ready, 1)
                if masked:
                    at_least(dve, inv_ready, n + 1)
                    at_least(dve, abs_done, n + 1)
                    dve.scalar_tensor_tensor(out=weight[:, g % 2, :], in0=row_abs[:, g % 2, :], scalar=0.0,
                                             in1=inv_sum[:, g % 2, :], op0=ALU.is_gt,
                                             op1=ALU.mult).then_inc(weight_ready, 1)

            def residual(t, p, g):
                n = t * G + g
                at_least(dve, op_ready, n + 1)
                at_least(dve, xb_ready, n + 1)
                at_least(dve, fin_ready, n - 1)
                dve.tensor_tensor(y[:, g % 2, :], o_bank[:, 0:D], xb[:, g % 2, :], ALU.add).then_inc(y_ready, 1)

            def moments(t, g):
                n = t * G + g
                at_least(dve, y_ready, n + 1)
                dve.bn_stats(stats[:, :], y[:, g % 2, :]).then_inc(stats_ready, 1)
                at_least_apart(dve, stats_ready, n + 1, dve_passed)
                dve.bn_aggr(mean_var[:, g % 2, :], stats[:, :]).then_inc(mean_var_ready, 1)

            def low_o(t, g):
                at_least(dve, o_high_done, t * G + g + 1)
                dve.tensor_tensor(oT[:, LOW, :, :].rearrange("p c k -> p (c k)"), o_bank[:, 0:OC * P],
                                  oT[:, HIGH, :, :].rearrange("p c k -> p (c k)").bitcast(F32),
                                  ALU.subtract).then_inc(o_low_done, 1)

            def low_staged(i, c):
                dve.wait_ge(xT_high, i * DC + c + 1)
                dve.tensor_tensor(xT[:, i, LOW, c, :], x_nat[:, i, :, :].rearrange("p g d -> p (g d)")[:, c * TOK:(c + 1) * TOK],
                                  xT[:, i, HIGH, c, :].bitcast(F32), ALU.subtract).then_inc(xT_low, 1)

            if given:
                low_w(0)
                for c in range(DC):
                    low_staged(0, c)
            for kind, i in FIRST:
                if (kind, i) == ("K", 0):
                    if not given:
                        low_w(0)
                    low_w(1)
                    dve.wait_ge(vectors_loaded, 16 * n_vectors)
                    if biased:
                        dve.wait_ge(bias_scaled, 1)
                if (kind, i) == ("K", 1):
                    low_w(2)
                    if DHP != DH:
                        dve.wait_ge(w_low, 3)
                        dve.memset(v[:, :, :, :, DH:DHP].rearrange("p a g h d -> p (a g h) d"), 0.0).then_inc(zeroed, 1)
                evacuate(0, 0, kind, i)
                if (kind, i) == ("V", 0):
                    add_adjacency(0, 0, 0, 0)
            if masked:
                largest(0, 0)
            weigh(0, 0)
            low_w(3)
            for c in range(DC):
                if given:
                    low_staged(1, c)

            def tile(t, pair, p):
                for g in range(G):
                    last = is_last(t)
                    final = last and g == G - 1
                    nt, npair, np_, ng = (t, pair, p, g + 1) if g < G - 1 else (t + 1, pair + p, 1 - p, 0)
                    if not final:
                        add_adjacency(nt, npair, np_, ng)
                    if not last:
                        for kind, i in EARLY[g]:
                            evacuate(t + 1, 1 - p, kind, i)
                    if g > 0:
                        residual(t, p, g - 1)
                        moments(t, g - 1)
                    elif not (isinstance(t, int) and t == 0):
                        residual(t - 1, 1 - p, G - 1)
                    if not last:
                        for kind, i in BEFORE[g]:
                            evacuate(t + 1, 1 - p, kind, i)
                    if g == 0 and not (isinstance(t, int) and t == 0):
                        moments(t - 1, G - 1)
                    if masked and not final:
                        largest(nt, ng)
                    if not final and given:
                        weigh(nt, ng)
                    if not last:
                        for kind, i in AFTER[g]:
                            evacuate(t + 1, 1 - p, kind, i)
                    if not final and not given:
                        weigh(nt, ng)
                    low_o(t, g)

            walk_tiles(dve, TILES, tile)
            residual(TILES - 1, 1, G - 1)
            moments(TILES - 1, G - 1)

        @block.gpsimd
        def _(pool):
            pool.memset(ident[:, :], 0.0).then_inc(const_made, 1)
            pool.wait_ge(const_made, 1)
            pool.affine_select(out=ident[:, :], in_=ident[:, :], compare_op=ALU.not_equal, fill=1.0,
                               base=0, pattern=[[-1, P]], channel_multiplier=1).then_inc(const_made, 1)
            for i in range(2):
                pool.memset(k_blk[:, i, :, :, :].rearrange("p s b k -> p (s b k)").bitcast(F32), 0.0).then_inc(blk_zeroed, 1)
            pool.wait_ge(zeroed, 1)
            pool.wait_ge(vectors_loaded, 16 * n_vectors)

            STEPS = 5 if rms else 3

            def add_bo(t, pair, p, g):
                n = t * G + g
                if g == 0:
                    at_least(pool, x_loaded[p], 16 * (pair + 1))
                at_least(pool, y_ready, n - 1)
                pool.tensor_tensor(xb[:, g % 2, :], x_nat[:, p, g, :], bo_b[:, :], ALU.add).then_inc(xb_ready, 1)

            def normalise(t, g):
                n = t * G + g
                at_least(pool, weight_ready, n + 1)
                for q in range(NB):
                    hs = slice(q * HB, (q + 1) * HB)
                    pool.tensor_tensor(probs[:, g % 2, hs, :], probs[:, g % 2, hs, :],
                                       weight[:, g % 2, hs].unsqueeze(2).to_broadcast([P, HB, P]),
                                       ALU.mult).then_inc(probs_ready, 1)

            def finish(t, g):
                n = t * G + g
                at_least(pool, mean_var_ready, n + 1)
                at_least_apart(pool, stored[g % 2], 16 * (t * 2 + g // 2), pool_passed)
                mean, var = mean_var[:, g % 2, 0:1], mean_var[:, g % 2, 1:2]
                done = n * STEPS
                if rms:
                    pool.tensor_tensor(scalars[:, 0:1], mean, mean, ALU.mult).then_inc(pool_step, 1)
                    at_least_apart(pool, pool_step, done + 1, pool_passed)
                    pool.tensor_scalar(scalars[:, 1:2], scalars[:, 0:1], var, RMS_EPS, ALU.add, ALU.add).then_inc(pool_step, 1)
                    done = done + 1
                else:
                    pool.tensor_scalar(scalars[:, 1:2], var, LN_EPS, None, ALU.add).then_inc(pool_step, 1)
                pool.wait_ge(pool_step, done + 1)
                pool.tensor_tensor(scalars[:, 2:3], scalars[:, 1:2], minus_half[:, :], ALU.pow).then_inc(pool_step, 1)
                at_least_apart(pool, pool_step, done + 2, pool_passed)
                if rms:
                    pool.tensor_tensor(o_nat[:, g % 2, :], y[:, g % 2, :], alpha_b[:, :], ALU.mult).then_inc(pool_step, 1)
                    at_least_apart(pool, pool_step, done + 3, pool_passed)
                    pool.tensor_scalar(o_nat[:, g % 2, :], o_nat[:, g % 2, :], scalars[:, 2:3], 1.0,
                                       ALU.mult, ALU.mult).then_inc(pool_step, 1)
                    at_least_apart(pool, pool_step, done + 4, pool_passed)
                    pool.tensor_tensor(o_nat[:, g % 2, :], o_nat[:, g % 2, :], gamma_b[:, :], ALU.add).then_inc(fin_ready, 1)
                else:
                    pool.tensor_scalar(scalars[:, 3:4], mean, scalars[:, 2:3], -1.0, ALU.mult, ALU.mult).then_inc(pool_step, 1)
                    at_least_apart(pool, pool_step, done + 3, pool_passed)
                    pool.tensor_scalar(o_nat[:, g % 2, :], y[:, g % 2, :], scalars[:, 2:3], scalars[:, 3:4],
                                       ALU.mult, ALU.add).then_inc(fin_ready, 1)

            def low_xT(t, p, c):
                at_least(pool, xT_high, (t + 2) * DC + c + 1)
                pool.tensor_tensor(xT[:, p, LOW, c, :], xT_raw[:, (p * DC + c) % 2, :], xT[:, p, HIGH, c, :].bitcast(F32),
                                   ALU.subtract).then_inc(xT_low, 1)

            normalise(0, 0)
            add_bo(0, 0, 0, 0)

            def tile(t, pair, p):
                for g in range(G):
                    if g > 0:
                        finish(t, g - 1)
                    elif not (isinstance(t, int) and t == 0):
                        finish(t - 1, G - 1)
                    if g < G - 1:
                        normalise(t, g + 1)
                        add_bo(t, pair, p, g + 1)
                    elif not is_last(t):
                        normalise(t + 1, 0)
                        add_bo(t + 1, pair + p, 1 - p, 0)
                    if given and g > 0 and not (isinstance(t, int) and t >= TILES - 2):
                        low_xT(t, p, g - 1)

            walk_tiles(pool, TILES, tile)
            finish(TILES - 1, G - 1)


def feed_forward_pass(nc, x_in, h_in, w1_in, b1_in, w2_in, b2_in, alpha_in, gamma_in, out,
                      x_nat, h_nat, h_loaded, first_piece, first_loaded, stored_before):
    TILES = x_in.shape[0] // G
    FF = w1_in.shape[1]
    FC = FF // P
    LAG = 2
    TURN = 6
    RING = 3
    with ExitStack() as ctx:
        def sb(name, shape, dt=F32):
            return ctx.enter_context(nc.sbuf_tensor(f"ff_{name}", shape, dt))

        def sem(name):
            return ctx.enter_context(nc.semaphore(f"ff_{name}"))

        ident = sb("ident", [P, P])
        w1 = sb("w1", [P, 2, DC, FF], F32R)
        w2 = sb("w2", [P, 2, FC, D], F32R)
        b1_c = sb("b1_c", [P, FC])
        b2_b = sb("b2_b", [P, D])
        alpha_b = sb("alpha_b", [P, D])
        gamma_b = sb("gamma_b", [P, D])
        hb = sb("hb", [P, 2, G, D])
        xg = sb("xg", [P, 2, G, D])
        hT = sb("hT", [P, 2, 2, DC, TOK], F32R)
        act_out = sb("act_out", [P, 2, TOK])
        gT = sb("gT", [P, RING, 2, TOK], F32R)
        y = sb("y", [P, G, D])
        z = sb("z", [P, G, D])
        o_nat = sb("o_nat", [P, G, D])
        stats = sb("stats", [P, 2, G, 6])
        mean_var = sb("mean_var", [P, 2, G, 2])
        ms = sb("ms", [P, 6, G])
        minus_half = sb("minus_half", [P, G])

        bank = ctx.enter_context(nc.psum_tensor("ff_bank", [P, 8, 512], F32))
        f_bank = bank[:, 0:2, :]
        x_bank = bank[:, 2:4, :]
        y_bank = bank[:, 4:8, :]

        b1_loaded = sem("b1_loaded")
        vectors_loaded = sem("vectors_loaded")
        const_made = sem("const_made")
        w_high = sem("w_high")
        w_low = sem("w_low")
        x_loaded = sem("x_loaded")
        stored = sem("stored")
        hT_psum = sem("hT_psum")
        f_ready = sem("f_ready")
        f2_done = sem("f2_done")
        y_psum = sem("y_psum")
        hT_high = sem("hT_high")
        hT_low = sem("hT_low")
        silu_done = sem("silu_done")
        g_high = sem("g_high")
        g_low = sem("g_low")
        y_ready = sem("y_ready")
        y_stats = sem("y_stats")
        y_moments = sem("y_moments")
        y_scaled = sem("y_scaled")
        z_ready = sem("z_ready")
        z_stats = sem("z_stats")
        z_moments = sem("z_moments")
        sums_ready = sem("sums_ready")
        pool_step = sem("pool_step")
        rms_ready = sem("rms_ready")
        shift_ready = sem("shift_ready")
        fin_ready = sem("fin_ready")
        dve_passed, pool_passed, sp_passed = sem("dve_passed"), sem("pool_passed"), sem("sp_passed")

        x_v = x_in.rearrange("(t g) p d -> t p g d", g=G)
        h_v = h_in.rearrange("(t g) p d -> t p g d", g=G)
        out_v = out.rearrange("(t g) p d -> t p g d", g=G)
        block = ctx.enter_context(nc.Block())
        is_last = lambda t: isinstance(t, int) and t == TILES - 1
        PC = D // P
        PIECES = 2 * FC // PC

        def as_stage(buf):
            return buf.rearrange("p g d -> p (g d)")[:, 0:PC * D].rearrange("p (c n) -> p c n", c=PC)

        stages = [first_piece[:, :, :], as_stage(hb[:, 1, :, :]), as_stage(xg[:, 1, :, :]), as_stage(o_nat[:, :, :]),
                  as_stage(y[:, :, :]), as_stage(z[:, :, :])]
        w1_v = w1_in.rearrange("(c p) n -> p c n", p=P)
        w2_v = w2_in.rearrange("(c p) n -> p c n", p=P)
        pieces = []
        for i in range(PIECES):
            k = (i // 2) * PC
            if i % 2 == 0:
                part, src = w1[:, :, :, k * P:(k + PC) * P], w1_v[:, :, k * P:(k + PC) * P]
            else:
                part, src = w2[:, :, k:k + PC, :], w2_v[:, k:k + PC, :]
            pieces.append((stages[i % len(stages)], part, src))
        w_loaded = [first_loaded] + [sem(f"w_loaded{i}") for i in range(1, PIECES)]
        SPLIT = [-1, -1] + [PC * (i // 2 - 1) + i % 2 for i in range(2, PIECES)]
        vectors = [(b2_b, b2_in), (gamma_b, gamma_in), (alpha_b, alpha_in)]

        @block.sync
        def _(sp):
            def load_piece(i):
                if i >= len(stages):
                    sp.wait_ge(w_low, i - len(stages) + 1)
                st, _, src = pieces[i]
                sp.dma_start(st, src).then_inc(w_loaded[i], 16)

            def load_x(t):
                sp.dma_start(x_nat[:, :, :], x_v[bass.ds(t, 1)].rearrange("a p g d -> p (a g) d")).then_inc(x_loaded, 16)

            with nc.allow_non_contiguous_dma(reason="bias column, 1536 elements once"):
                sp.dma_start(b1_c[:, :], b1_in.rearrange("(c p) -> p c", p=P)).then_inc(b1_loaded, 16)
            for i in range(1, 4):
                load_piece(i)
            for dst, src in vectors:
                sp.dma_start(dst[:, :], src.rearrange("(a d) -> a d", a=1).to_broadcast([P, D])).then_inc(vectors_loaded, 16)
            for done in stored_before:
                sp.wait_ge(done, 16 * TILES * G // 2)
            load_x(0)
            for i in range(4, PIECES):
                load_piece(i)

            def load(t):
                sp.dma_start(h_nat[:, :, :], h_v[bass.ds(t, 1)].rearrange("a p g d -> p (a g) d")).then_inc(h_loaded, 16)
                load_x(t)

            def tile(t, pair, p):
                if not is_last(t):
                    at_least_apart(sp, hT_psum, (t + 1) * DC, sp_passed)
                    at_least_apart(sp, sums_ready, 2 * (t + 1), sp_passed)
                    load(t + 1)
                if not (isinstance(t, int) and t == 0):
                    at_least_apart(sp, fin_ready, t * G, sp_passed)
                    sp.dma_start(out_v[bass.ds(t - 1, 1)].rearrange("a p g d -> p (a g) d"), o_nat[:, :, :]).then_inc(stored, 16)

            walk_tiles(sp, TILES, tile)
            sp.wait_ge(fin_ready, TILES * G)
            sp.dma_start(out_v[TILES - 1], o_nat[:, :, :]).then_inc(stored, 16)
            sp.wait_ge(stored, 16 * TILES)

        @block.tensor
        def _(pe):
            def turn(t, p, c):
                if c == 0:
                    at_least(pe, h_loaded, 16 * (t + 1))
                at_least(pe, hT_low, t * DC + c - 1)
                for g in range(G):
                    mm = pe.transpose(x_bank[:, (p + c) % 2, g * P:(g + 1) * P], h_nat[:, g, c * P:(c + 1) * P], ident[:, :])
                mm.then_inc(hT_psum, 1)

            def first(t, p, m):
                if m == 0:
                    at_least(pe, hT_low, (t + 1) * DC)
                if isinstance(t, int) and t == 0 and m % PC == 0:
                    pe.wait_ge(w_low, 2 * (m // PC) + 1)
                at_least(pe, silu_done, t * FC + m - 1)
                todo = [(c, a, b) for c in range(DC) for a, b in PARTS]
                for k, (c, a, b) in enumerate(todo):
                    mm = pe.matmul(f_bank[:, m % 2, :], w1[:, a, c, m * P:(m + 1) * P], hT[:, p, b, c, :],
                                   start=k == 0, stop=k == len(todo) - 1)
                mm.then_inc(f_ready, 1)

            def second(t, m):
                at_least(pe, g_low, t * FC + m + 1)
                if isinstance(t, int) and t == 0 and m % PC == 0:
                    pe.wait_ge(w_low, 2 * (m // PC) + 2)
                for g in range(G):
                    if m == 0:
                        at_least(pe, y_ready, (t - 1) * G + g + 1)
                    for k, (a, b) in enumerate(PARTS):
                        mm = pe.matmul(y_bank[:, g, 0:D], gT[:, m % RING, a, g * P:(g + 1) * P], w2[:, b, m, :],
                                       start=m == 0 and k == 0, stop=m == FC - 1 and k == 2)
                    if m == FC - 1 and g < G - 1:
                        mm.then_inc(y_psum, 1)
                if m == FC - 1:
                    mm.then_inc(y_psum, 1)
                else:
                    mm.then_inc(f2_done, 1)

            pe.wait_ge(const_made, 2)
            for c in range(DC):
                turn(0, 0, c)

            def tile(t, pair, p):
                for m in range(FC):
                    first(t, p, m)
                    if m >= LAG:
                        second(t, m - LAG)
                    elif not (isinstance(t, int) and t == 0):
                        second(t - 1, FC + m - LAG)
                    if TURN <= m < TURN + DC and not is_last(t):
                        turn(t + 1, 1 - p, m - TURN)

            walk_tiles(pe, TILES, tile)
            for m in range(FC - LAG, FC):
                second(TILES - 1, m)

        @block.scalar
        def _(act):
            def high_pieces(step):
                for i, (st, dst, _) in enumerate(pieces):
                    if SPLIT[i] == step:
                        act.wait_ge(w_loaded[i], 16)
                        act.activation(dst[:, HIGH], st, ACT.Copy).then_inc(w_high, 1)

            def high_hT(t, p, c):
                at_least(act, hT_psum, t * DC + c + 1)
                act.activation(hT[:, p, HIGH, c, :], x_bank[:, (p + c) % 2, :], ACT.Copy).then_inc(hT_high, 1)

            for c in range(DC):
                high_hT(0, 0, c)
            high_pieces(-1)
            act.wait_ge(b1_loaded, 16)

            def tile(t, pair, p):
                for m in range(FC):
                    n = t * FC + m
                    at_least(act, f_ready, n + 1)
                    at_least(act, g_low, n - 1)
                    act.activation(act_out[:, m % 2, :], f_bank[:, m % 2, :], ACT.Silu,
                                   bias=b1_c[:, m:m + 1]).then_inc(silu_done, 1)
                    at_least(act, silu_done, n + 1)
                    act.activation(gT[:, m % RING, HIGH, :], act_out[:, m % 2, :], ACT.Copy).then_inc(g_high, 1)
                    if isinstance(t, int) and t == 0:
                        high_pieces(m)
                    if TURN <= m < TURN + DC and not is_last(t):
                        high_hT(t + 1, 1 - p, m - TURN)

            walk_tiles(act, TILES, tile)

        @block.vector
        def _(dve):
            dve.memset(minus_half[:, :], -0.5).then_inc(const_made, 1)

            def low_pieces(step):
                for i, (st, dst, _) in enumerate(pieces):
                    if SPLIT[i] == step:
                        dve.wait_ge(w_high, i + 1)
                        dve.tensor_tensor(dst[:, LOW], st, dst[:, HIGH].bitcast(F32), ALU.subtract).then_inc(w_low, 1)

            def low_hT(t, p, c):
                at_least(dve, hT_high, t * DC + c + 1)
                dve.tensor_tensor(hT[:, p, LOW, c, :], x_bank[:, (p + c) % 2, :],
                                  hT[:, p, HIGH, c, :].bitcast(F32), ALU.subtract).then_inc(hT_low, 1)

            for c in range(DC):
                low_hT(0, 0, c)
            low_pieces(-1)

            def moments(src, which, g, ready, count, stats_done, done):
                at_least(dve, ready, count)
                dve.bn_stats(stats[:, which, g, :], src[:, g, :]).then_inc(stats_done, 1)
                at_least_apart(dve, stats_done, count, dve_passed)
                dve.bn_aggr(mean_var[:, which, g, :], stats[:, which, g, :]).then_inc(done, 1)

            def add_residual(t, p, g):
                at_least(dve, y_psum, t * G + g + 1)
                at_least(dve, sums_ready, 2 * t + 1)
                dve.tensor_tensor(y[:, g, :], y_bank[:, g, 0:D], hb[:, p, g, :], ALU.add).then_inc(y_ready, 1)

            def second_sum(t, p, g):
                at_least(dve, rms_ready, t + 1)
                at_least(dve, sums_ready, 2 * t + 2)
                at_least(dve, fin_ready, t * G)
                dve.scalar_tensor_tensor(out=z[:, g, :], in0=y[:, g, :], scalar=ms[:, 2, g:g + 1], in1=alpha_b[:, :],
                                         op0=ALU.mult, op1=ALU.mult).then_inc(y_scaled, 1)
                at_least(dve, y_scaled, t * G + g + 1)
                dve.tensor_tensor(z[:, g, :], z[:, g, :], xg[:, p, g, :], ALU.add).then_inc(z_ready, 1)

            def after(t, p, step):
                if step == 1:
                    for g in range(G):
                        add_residual(t, p, g)
                elif step == 2:
                    for g in range(G):
                        moments(y, 0, g, y_ready, t * G + g + 1, y_stats, y_moments)
                elif 4 <= step < 4 + G:
                    second_sum(t, p, step - 4)
                    moments(z, 1, step - 4, z_ready, t * G + step - 4 + 1, z_stats, z_moments)

            def tile(t, pair, p):
                for m in range(FC):
                    n = t * FC + m
                    at_least(dve, g_high, n + 1)
                    dve.tensor_tensor(gT[:, m % RING, LOW, :], act_out[:, m % 2, :],
                                      gT[:, m % RING, HIGH, :].bitcast(F32), ALU.subtract).then_inc(g_low, 1)
                    if isinstance(t, int) and t == 0:
                        low_pieces(m)
                    if TURN <= m < TURN + DC and not is_last(t):
                        low_hT(t + 1, 1 - p, m - TURN)
                    if not (isinstance(t, int) and t == 0):
                        after(t - 1, 1 - p, m)

            walk_tiles(dve, TILES, tile)
            for step in range(FC):
                after(TILES - 1, 1, step)

        @block.gpsimd
        def _(pool):
            pool.memset(ident[:, :], 0.0).then_inc(pool_step, 1)
            pool.wait_ge(pool_step, 1)
            pool.affine_select(out=ident[:, :], in_=ident[:, :], compare_op=ALU.not_equal, fill=1.0,
                               base=0, pattern=[[-1, P]], channel_multiplier=1).then_inc(const_made, 1)
            pool.wait_ge(vectors_loaded, 16 * len(vectors))
            pool.wait_ge(const_made, 2)
            STEPS = 5

            def sums(t, p):
                at_least(pool, h_loaded, 16 * (t + 1))
                at_least(pool, y_ready, G * (t - 1))
                pool.tensor_tensor(hb[:, p, :, :], h_nat[:, :, :], b2_b[:, :].unsqueeze(1).to_broadcast([P, G, D]),
                                   ALU.add).then_inc(sums_ready, 1)
                at_least(pool, x_loaded, 16 * (t + 1))
                at_least(pool, z_ready, G * (t - 1))
                pool.tensor_tensor(xg[:, p, :, :], x_nat[:, :, :], gamma_b[:, :].unsqueeze(1).to_broadcast([P, G, D]),
                                   ALU.add).then_inc(sums_ready, 1)

            def norms(t):
                done = 1 + t * STEPS
                at_least(pool, y_moments, (t + 1) * G)
                mean, var = mean_var[:, 0, :, 0], mean_var[:, 0, :, 1]
                pool.tensor_tensor(ms[:, 0, :], mean, mean, ALU.mult).then_inc(pool_step, 1)
                at_least(pool, pool_step, done + 1)
                pool.tensor_tensor(ms[:, 1, :], ms[:, 0, :], var, ALU.add).then_inc(pool_step, 1)
                at_least_apart(pool, pool_step, done + 2, pool_passed)
                pool.tensor_scalar(ms[:, 0, :], ms[:, 1, :], RMS_EPS, None, ALU.add).then_inc(pool_step, 1)
                at_least(pool, pool_step, done + 3)
                at_least(pool, y_scaled, t * G)
                pool.tensor_tensor(ms[:, 2, :], ms[:, 0, :], minus_half[:, :], ALU.pow).then_inc(rms_ready, 1)
                at_least_apart(pool, z_moments, (t + 1) * G, pool_passed)
                mean, var = mean_var[:, 1, :, 0], mean_var[:, 1, :, 1]
                pool.tensor_scalar(ms[:, 3, :], var, LN_EPS, None, ALU.add).then_inc(pool_step, 1)
                at_least(pool, pool_step, done + 4)
                pool.tensor_tensor(ms[:, 4, :], ms[:, 3, :], minus_half[:, :], ALU.pow).then_inc(pool_step, 1)
                at_least_apart(pool, pool_step, done + 5, pool_passed)

            def finish(t, g):
                mean = mean_var[:, 1, g, 0:1]
                at_least_apart(pool, stored, 16 * t, pool_passed)
                pool.tensor_scalar(ms[:, 5, g:g + 1], mean, ms[:, 4, g:g + 1], -1.0, ALU.mult, ALU.mult).then_inc(shift_ready, 1)
                at_least_apart(pool, shift_ready, t * G + g + 1, pool_passed)
                pool.tensor_scalar(o_nat[:, g, :], z[:, g, :], ms[:, 4, g:g + 1], ms[:, 5, g:g + 1],
                                   ALU.mult, ALU.add).then_inc(fin_ready, 1)

            sums(0, 0)

            def tile(t, pair, p):
                if not (isinstance(t, int) and t == 0):
                    norms(t - 1)
                    for g in range(G):
                        finish(t - 1, g)
                if isinstance(t, int) and t == 0:
                    pool.wait_ge(w_low, PIECES)
                if not is_last(t):
                    sums(t + 1, 1 - p)

            walk_tiles(pool, TILES, tile)
            norms(TILES - 1)
            for g in range(G):
                finish(TILES - 1, g)


def build(nc, x, xT, adj, q0, k0, v0, bv0, o0, bo0, q1, bq1, k1, bk1, v1, bv1, o1, bo1,
          w1, b1, w2, b2, alpha1, gamma1, alpha2, gamma2, out):
    x1 = nc.dram_tensor("x1", x.shape, F32, kind="Internal").ap()
    h1 = nc.dram_tensor("h1", x.shape, F32, kind="Internal").ap()
    with ExitStack() as ctx:
        def sb(name, shape):
            return ctx.enter_context(nc.sbuf_tensor(name, shape, F32))

        def sem(name):
            return ctx.enter_context(nc.semaphore(name))

        x_nat = sb("x_nat", [P, 2, G, D])
        x_loaded = [[sem(f"x_loaded{a}{i}") for i in range(2)] for a in range(2)]
        x1_stored = [sem(f"x1_stored{i}") for i in range(2)]
        h1_stored = [sem(f"h1_stored{i}") for i in range(2)]
        ahead = [(x_nat[:, 0, :, :], x1[0:G].rearrange("g p d -> p g d"), x_loaded[1][0])]
        attention_pass(nc, "a0", x, xT, adj, q0, k0, v0, o0, None, None, bv0, bo0, None, None, x1, 12, True,
                       x_nat, x_loaded[0], False, ahead, x1_stored, ())
        h_nat = sb("h_nat", [P, G, D])
        w1_piece = sb("w1_piece", [P, DC, D])
        h_loaded = sem("h_loaded")
        piece_loaded = sem("piece_loaded")
        ahead = [(h_nat[:, :, :], h1[0:G].rearrange("g p d -> p g d"), h_loaded),
                 (w1_piece[:, :, :], w1.rearrange("(c p) n -> p c n", p=P)[:, :, 0:D], piece_loaded)]
        attention_pass(nc, "a1", x1, None, adj, q1, k1, v1, o1, bq1, bk1, bv1, bo1, alpha1, gamma1, h1, 8, False,
                       x_nat, x_loaded[1], True, ahead, h1_stored, x1_stored)
        feed_forward_pass(nc, x1, h1, w1, b1, w2, b2, alpha2, gamma2, out,
                          x_nat[:, 0, :, :], h_nat, h_loaded, w1_piece, piece_loaded, h1_stored)


_INS = ['x', 'x_turned', 'adj', 'L0_gnn_Wq', 'L0_gnn_Wk', 'L0_gnn_Wv', 'L0_gnn_bv', 'L0_gnn_Wo', 'L0_gnn_bo',
        'L1_gnn_wq', 'L1_gnn_bq', 'L1_gnn_wk', 'L1_gnn_bk', 'L1_gnn_wv', 'L1_gnn_bv', 'L1_gnn_wo', 'L1_gnn_bo',
        'L1_gnn_w1', 'L1_gnn_b1', 'L1_gnn_w2', 'L1_gnn_b2', 'L1_gnn_alpha1', 'L1_gnn_gamma1',
        'L1_gnn_alpha2', 'L1_gnn_gamma2']
_TURNED = ['L0_gnn_Wq', 'L0_gnn_Wk', 'L0_gnn_Wv', 'L0_gnn_Wo']


def kernel(**inputs):
    import numpy as _np
    import concourse.bacc as _bacc
    from concourse import mybir as _mybir
    from concourse.bass_utils import run_bass_kernel_spmd as _run

    nc = _bacc.Bacc("TRN2", target_bir_lowering=False, num_devices=1)
    arrays, args = {}, []
    for name in _INS:
        a = _np.asarray(inputs["x"]).reshape(-1, 384).T if name == "x_turned" else _np.asarray(inputs[name])
        a = _np.ascontiguousarray(a.T if name in _TURNED else a)
        arrays[f"in_{name}_dram"] = a
        args.append(nc.dram_tensor(f"in_{name}_dram", a.shape, _mybir.dt.from_np(a.dtype), kind="ExternalInput").ap())
    args.append(nc.dram_tensor("out_dram", (64, 128, 384), _mybir.dt.float32, kind="ExternalOutput").ap())
    build(nc, *args)
    r = _run(nc, [arrays], core_ids=[0])
    return r.results[0]["out_dram"]
```
